# Optimizing a Trainium2 kernel written in Bass

```python
import numpy as np
import jax
import jax.numpy as jnp

def _softmax(x, axis=-1):
    return jax.nn.softmax(x, axis=axis)

def _gelu(x):
    return jax.nn.gelu(x, approximate=True)

def _silu(x):
    return jax.nn.silu(x)

def _sigmoid(x):
    return jax.nn.sigmoid(x)

def _layernorm(x, axis=-1, eps=1e-05):
    m = jnp.mean(x, axis=axis, keepdims=True)
    v = jnp.var(x, axis=axis, keepdims=True)
    return (x - m) / jnp.sqrt(v + eps)

def _scatter_add(tgt, idx, src, axis=0):
    return tgt.at[idx].add(src)

def _segment_sum(src, seg, n):
    return jax.ops.segment_sum(src, seg, n)
kernel_name = 'mk_macaron_d1_jaxref_r8_10580e'

def setup_inputs(seed: int=0):
    np.random.seed(seed)
    _w = jnp.asarray

    def _L0_attn_setup():
        import jax, jax.numpy as jnp
        import numpy as np
        B, L, D, N, K = (2, 256, 128, 16, 4)
        LN_EPS = 1e-05

        def _mamba_block(x, W_in, W_conv, b_conv, W_xproj, W_dt, b_dt, A_log, ln_gamma, ln_beta, W_out, b_out):
            d = x.shape[-1]
            n = A_log.shape[-1]
            k = W_conv.shape[-1]
            x_res = x
            xz = x @ W_in.T
            x_in, z = (xz[..., :d], xz[..., d:])
            xc = jax.lax.conv_general_dilated(x_in.transpose(0, 2, 1), W_conv, window_strides=(1,), padding=[(k - 1, 0)], feature_group_count=d, dimension_numbers=('NCH', 'OIH', 'NCH')) + b_conv[None, :, None]
            x_conv = xc.transpose(0, 2, 1)
            gate = jax.nn.silu(x_conv) * z
            A = -jnp.exp(A_log)
            delta = jax.nn.softplus(gate @ W_dt.T + b_dt)
            BC = gate @ W_xproj.T
            B_p, C_p = (BC[..., :n], BC[..., n:])
            delta_A = jnp.exp(jnp.einsum('bld,dn->bldn', delta, A))
            delta_B_x = jnp.einsum('bld,bln,bld->bldn', delta, B_p, gate)

            def step(h, inp):
                a, bx = inp
                h = a * h + bx
                return (h, h)
            h0 = jnp.zeros((x.shape[0], d, n), x.dtype)
            _, hs = jax.lax.scan(step, h0, (delta_A.transpose(1, 0, 2, 3), delta_B_x.transpose(1, 0, 2, 3)))
            y = jnp.einsum('lbdn,bln->bld', hs, C_p)
            y = y + x_res
            mu = y.mean(-1, keepdims=True)
            var = ((y - mu) ** 2).mean(-1, keepdims=True)
            y = (y - mu) / jnp.sqrt(var + LN_EPS) * ln_gamma + ln_beta
            return y @ W_out.T + b_out
        key = jax.random.key(seed)
        ks = jax.random.split(key, 8)

        def w(k, shape, sc=0.02):
            return jax.random.normal(k, shape, dtype=jnp.float32) * sc
        x = jax.random.normal(ks[0], (B, L, D), dtype=jnp.float32)
        W_in = w(ks[1], (2 * D, D))
        W_conv = w(ks[2], (D, 1, K))
        b_conv = jnp.zeros((D,), jnp.float32)
        W_xproj = w(ks[3], (2 * N, D))
        W_dt = w(ks[4], (D, D))
        b_dt = jnp.zeros((D,), jnp.float32)
        A_log = jnp.log(jnp.tile(jnp.arange(1, N + 1, dtype=jnp.float32), (D, 1)))
        ln_gamma = jnp.ones((D,), jnp.float32)
        ln_beta = jnp.zeros((D,), jnp.float32)
        W_out = w(ks[5], (D, D))
        b_out = jnp.zeros((D,), jnp.float32)
        return dict(x=x, W_in=W_in, W_conv=W_conv, b_conv=b_conv, W_xproj=W_xproj, W_dt=W_dt, b_dt=b_dt, A_log=A_log, ln_gamma=ln_gamma, ln_beta=ln_beta, W_out=W_out, b_out=b_out)
    _L0_attn_in = _L0_attn_setup()

    def _L0_ffn_setup():
        import jax, jax.numpy as jnp
        import numpy as np
        H = 128
        F = 512
        E = 8
        TOP_K = 2
        B, S = (1, 256)
        key = jax.random.key(seed)
        k0, k1, k2, k3 = jax.random.split(key, 4)
        hidden_states = jax.random.normal(k0, (B, S, H), dtype=jnp.float32)
        gate_w = jax.random.normal(k1, (E, H), dtype=jnp.float32) * 0.02
        gate_up_w = jax.random.normal(k2, (E, 2 * F, H), dtype=jnp.float32) * 0.02
        down_w = jax.random.normal(k3, (E, H, F), dtype=jnp.float32) * 0.02
        return {'hidden_states': hidden_states, 'gate_w': gate_w, 'gate_up_w': gate_up_w, 'down_w': down_w}
    _L0_ffn_in = _L0_ffn_setup()
    _d = {'L0_attn_x': _L0_attn_in['x'], 'L0_attn_W_in': _L0_attn_in['W_in'], 'L0_attn_W_conv': _L0_attn_in['W_conv'], 'L0_attn_b_conv': _L0_attn_in['b_conv'], 'L0_attn_W_xproj': _L0_attn_in['W_xproj'], 'L0_attn_W_dt': _L0_attn_in['W_dt'], 'L0_attn_b_dt': _L0_attn_in['b_dt'], 'L0_attn_A_log': _L0_attn_in['A_log'], 'L0_attn_ln_gamma': _L0_attn_in['ln_gamma'], 'L0_attn_ln_beta': _L0_attn_in['ln_beta'], 'L0_attn_W_out': _L0_attn_in['W_out'], 'L0_attn_b_out': _L0_attn_in['b_out'], 'L0_ffn_gate_w': _L0_ffn_in['gate_w'], 'L0_ffn_gate_up_w': _L0_ffn_in['gate_up_w'], 'L0_ffn_down_w': _L0_ffn_in['down_w']}
    _x0 = _d['L0_attn_x']
    _d['L0_attn_x'] = jax.random.normal(jax.random.fold_in(jax.random.key(seed), 1), (8, 256, 128), dtype=_x0.dtype)
    del _x0
    return _d

def reference(L0_attn_x, L0_attn_W_in, L0_attn_W_conv, L0_attn_b_conv, L0_attn_W_xproj, L0_attn_W_dt, L0_attn_b_dt, L0_attn_A_log, L0_attn_ln_gamma, L0_attn_ln_beta, L0_attn_W_out, L0_attn_b_out, L0_ffn_gate_w, L0_ffn_gate_up_w, L0_ffn_down_w):

    def _L0_attn_ref(x, W_in, W_conv, b_conv, W_xproj, W_dt, b_dt, A_log, ln_gamma, ln_beta, W_out, b_out):
        import jax, jax.numpy as jnp
        import numpy as np
        B, L, D, N, K = (2, 256, 128, 16, 4)
        LN_EPS = 1e-05

        def _mamba_block(x, W_in, W_conv, b_conv, W_xproj, W_dt, b_dt, A_log, ln_gamma, ln_beta, W_out, b_out):
            d = x.shape[-1]
            n = A_log.shape[-1]
            k = W_conv.shape[-1]
            x_res = x
            xz = x @ W_in.T
            x_in, z = (xz[..., :d], xz[..., d:])
            xc = jax.lax.conv_general_dilated(x_in.transpose(0, 2, 1), W_conv, window_strides=(1,), padding=[(k - 1, 0)], feature_group_count=d, dimension_numbers=('NCH', 'OIH', 'NCH')) + b_conv[None, :, None]
            x_conv = xc.transpose(0, 2, 1)
            gate = jax.nn.silu(x_conv) * z
            A = -jnp.exp(A_log)
            delta = jax.nn.softplus(gate @ W_dt.T + b_dt)
            BC = gate @ W_xproj.T
            B_p, C_p = (BC[..., :n], BC[..., n:])
            delta_A = jnp.exp(jnp.einsum('bld,dn->bldn', delta, A))
            delta_B_x = jnp.einsum('bld,bln,bld->bldn', delta, B_p, gate)

            def step(h, inp):
                a, bx = inp
                h = a * h + bx
                return (h, h)
            h0 = jnp.zeros((x.shape[0], d, n), x.dtype)
            _, hs = jax.lax.scan(step, h0, (delta_A.transpose(1, 0, 2, 3), delta_B_x.transpose(1, 0, 2, 3)))
            y = jnp.einsum('lbdn,bln->bld', hs, C_p)
            y = y + x_res
            mu = y.mean(-1, keepdims=True)
            var = ((y - mu) ** 2).mean(-1, keepdims=True)
            y = (y - mu) / jnp.sqrt(var + LN_EPS) * ln_gamma + ln_beta
            return y @ W_out.T + b_out
        return _mamba_block(x, W_in, W_conv, b_conv, W_xproj, W_dt, b_dt, A_log, ln_gamma, ln_beta, W_out, b_out)

    def _L0_ffn_ref(hidden_states, gate_w, gate_up_w, down_w):
        import jax, jax.numpy as jnp
        import numpy as np
        H = 128
        F = 512
        E = 8
        TOP_K = 2
        B, S = (1, 256)
        b, s, h = hidden_states.shape
        x = hidden_states.reshape(-1, h)
        router_logits = x @ gate_w.T
        probs = jax.nn.softmax(router_logits.astype(jnp.float32), axis=-1)
        topw, sel = jax.lax.top_k(probs, TOP_K)
        topw = topw / jnp.sum(topw, axis=-1, keepdims=True)
        topw = topw.astype(x.dtype)
        combine = jnp.sum(jax.nn.one_hot(sel, E, dtype=x.dtype) * topw[..., None], axis=1)
        gu = jnp.einsum('th,efh->etf', x, gate_up_w)
        gate, up = (gu[..., :F], gu[..., F:])
        hact = up * jax.nn.gelu(gate, approximate=False)
        expert_out = jnp.einsum('etf,ehf->eth', hact, down_w)
        out = jnp.einsum('eth,te->th', expert_out, combine)
        return out.reshape(b, s, h)
    x = L0_attn_x
    x = x + 0.5 * _L0_ffn_ref(_layernorm(x, axis=-1), L0_ffn_gate_w, L0_ffn_gate_up_w, L0_ffn_down_w)
    x = x + _L0_attn_ref(_layernorm(x, axis=-1), L0_attn_W_in, L0_attn_W_conv, L0_attn_b_conv, L0_attn_W_xproj, L0_attn_W_dt, L0_attn_b_dt, L0_attn_A_log, L0_attn_ln_gamma, L0_attn_ln_beta, L0_attn_W_out, L0_attn_b_out)
    x = x + 0.5 * _L0_ffn_ref(_layernorm(x, axis=-1), L0_ffn_gate_w, L0_ffn_gate_up_w, L0_ffn_down_w)
    return x

_drawn_inputs = setup_inputs


def setup_inputs(seed=0):
    import zlib

    import numpy as np

    out = dict(_drawn_inputs(seed))
    spreads = {'L0_attn_b_conv': (0.0, 0.8),
     'L0_attn_b_dt': (0.0, 0.8),
     'L0_attn_ln_gamma': (1.0, 0.2),
     'L0_attn_ln_beta': (0.0, 0.322),
     'L0_attn_b_out': (0.0, 0.1)}
    factors = {'L0_attn_W_in': 8.0,
     'L0_attn_W_conv': 8.0,
     'L0_attn_W_xproj': 8.0,
     'L0_attn_W_dt': 8.0,
     'L0_attn_A_log': 8.0,
     'L0_ffn_gate_w': 8.0,
     'L0_ffn_gate_up_w': 7.05,
     'L0_ffn_down_w': 7.071}
    for name, (base, spread) in spreads.items():
        noise = np.random.default_rng([zlib.crc32(name.encode()), seed]).standard_normal(out[name].shape)
        drawn = base * np.exp(spread * noise) if base else spread * noise
        out[name] = jnp.asarray(drawn.astype(out[name].dtype))
    for name, factor in factors.items():
        out[name] = (out[name] * factor).astype(out[name].dtype)
    return out
```

```python
from contextlib import ExitStack

import concourse.bass as bass
from concourse import mybir

ALU = mybir.AluOpType
ACT = mybir.ActivationFunctionType
AX = mybir.AxisListType
F32 = mybir.dt.float32
F32R = mybir.dt.float32r
BF16 = mybir.dt.bfloat16
I32 = mybir.dt.int32
U32 = mybir.dt.uint32

P = 128
B, L, D = 8, 256, 128
T = B * L
C = T // P
GROUPS, GC = 4, C // 4
GT = GC * P
E, F, TOPK = 8, 512, 2
FC = F // P
J = TOPK * C
NT = (T * TOPK - E) // P + E
RING = 3
LOOPS = (NT - RING) // RING
WCOLS = 2 * F + FC * D
N = 16
TAPS = 4
PAD = TAPS
BLEN = L + PAD
EPS = 1e-5
BC_PARTS = 3
BCR = BC_PARTS * 2 * N
LAG = 4

K_IOTA, K_TRI, K_CENTRE, K_IDENT = 0, P, 2 * P, 3 * P
K_TILE = 4 * P
K_JP1 = K_TILE + C
K_P = K_JP1 + J
K_SEL = K_P + 1
K_COLS = K_SEL + 2 * N
V_BCONV, V_BDT, V_GAMMA, V_BETA, V_CONV = 0, 1, 2, 3, 4
V_ALOG = V_CONV + TAPS
V_COLS = V_ALOG + N
M_INX, M_INZ, M_DT, M_OUT, M_BOUT, M_BC = 0, D, 2 * D, 3 * D, 4 * D, 5 * D
M_GATE = M_BC + BCR
M_COLS = M_GATE + E

assert (NT - RING) % RING == 0


def macaron_block(nc, x_in, experts_in, consts_in, vectors_in, mats_in, out):
    with ExitStack() as ctx:
        def sb(name, shape, dt=F32):
            return ctx.enter_context(nc.sbuf_tensor(name, shape, dt))

        def sem(name):
            return ctx.enter_context(nc.semaphore(name))

        xn_dram = [nc.dram_tensor(f"xn_rows_{l}", (T, D), F32).ap() for l in range(2)]
        y_dram = [nc.dram_tensor(f"expert_rows_{l}", (TOPK * T, D), F32).ap() for l in range(2)]

        ps = ctx.enter_context(nc.psum_tensor("ps", [P, 8, 512], F32))

        consts = sb("consts", [P, K_COLS])
        vectors = sb("vectors", [P, V_COLS])
        mats = sb("mats", [P, M_COLS])
        ident = consts[:, K_IDENT:K_IDENT + P]
        tri_b = sb("tri_b", [P, P], BF16)
        ones_b = sb("ones_b", [P, P], BF16)
        sel_b = sb("sel_b", [P, 2 * N], BF16)
        ones_f = sb("ones_f", [P, E])
        staging = sb("staging", [P, 2, WCOLS])
        w_hi = sb("w_hi", [P, E, WCOLS], F32R)
        w_lo = sb("w_lo", [P, E, WCOLS], F32R)
        conv_rows = sb("conv_rows", [P, TAPS, P])
        conv_w = sb("conv_w", [P, TAPS, P])
        out_g = sb("out_g", [P, P])
        out_w = sb("out_w", [P, P])
        out_c = sb("out_c", [P, P])
        beta_b = sb("beta_b", [P, P])
        neg_a = sb("neg_a", [P, N])

        x = sb("x", [P, C, D])
        xn = sb("xn", [P, C, D])
        xnT = sb("xnT", [P, B, BLEN])
        stats = sb("stats", [P, C, 6])
        mv = sb("mv", [P, C, 2])
        var_e = sb("var_e", [P, C])
        ln_v = sb("ln_v", [P, C])
        rstd0 = sb("rstd0", [P, C])
        nt0 = sb("nt0", [P, C])
        nt1 = sb("nt1", [P, C])
        rstd = sb("rstd", [P, C])

        lg = sb("lg", [P, C, E])
        shared = sb("shared", [P, max(8 * GT, C * E * E + (T // GROUPS) * TOPK + 3 * J * NT // 2)])
        beats = shared[:, 0:C * E * E].rearrange("p (c e o) -> p c e o", c=C, e=E)
        rank = sb("rank", [P, C, E])
        top = sb("top", [P, TOPK, C, E])
        picked = sb("picked", [P, C + 1, E], BF16)
        prod = sb("prod", [P, TOPK, C, E])
        lsel = sb("lsel", [P, TOPK, C])
        ldiff = sb("ldiff", [P, C])
        e2 = sb("e2", [P, C])
        den = sb("den", [P, C])
        half_w = sb("half_w", [P, TOPK, C])
        over = sb("over", [P, E, C])
        ntile = sb("ntile", [P, E])
        tile_end = sb("tile_end", [P, E])
        base = sb("base", [P, E])
        slot = sb("slot", [P, C, E])
        slot_f = sb("slot_f", [P, J])
        slot_i = sb("slot_i", [P, J], I32)
        tile_i = sb("tile_i", [P, J], I32)
        row_i = sb("row_i", [P, J], I32)
        tile_f = sb("tile_f", [P, J])
        row_f = sb("row_f", [P, J])
        JP = J // GROUPS
        at_row, at_tile = C * E * E, C * E * E + JP * P
        at_ids = at_tile + J * NT // 2
        in_row = shared[:, at_row:at_tile].bitcast(BF16).rearrange("p (a j r) -> p a j r", a=2, j=JP)
        in_tile = shared[:, at_tile:at_ids].bitcast(BF16).rearrange("p (j t) -> p j t", j=J)
        ids_rhs = shared[:, at_ids:at_ids + J * NT].bitcast(BF16).rearrange("p (j v t) -> p j v t", j=J, v=2)
        ids = sb("ids", [P, 2, NT])
        id128 = sb("id128", [P, NT])
        empty = sb("empty", [P, NT])
        put_i = sb("put_i", [P, NT], I32)
        get_i = sb("get_i", [P, NT], I32)
        le_end = sb("le_end", [P, NT, E])
        exp_f = sb("exp_f", [P, NT])
        exp_i = sb("exp_i", [P, NT], I32)

        xg = sb("xg", [P, RING, D])
        xT_hi = sb("xT_hi", [P, RING, P], F32R)
        xT_lo = sb("xT_lo", [P, RING, P], F32R)
        gelu = sb("gelu", [P, F])
        hact = sb("hact", [P, F])
        hT_hi = sb("hT_hi", [P, F], F32R)
        hT_lo = sb("hT_lo", [P, F], F32R)
        ysb = sb("ysb", [P, RING, D])
        ybuf = staging[:].rearrange("p a b -> p (a b)")[:, 0:3 * 2 * GC * D].rearrange(
            "p (r k c d) -> p r k c d", r=3, k=TOPK, c=GC)

        gate = sb("gate", [P, T])
        delta = xn[:].rearrange("p c d -> p (c d)")
        hc = shared[:, 0:4 * GT].rearrange("p (r t) -> p r t", r=4)
        silu = shared[:, 4 * GT:6 * GT].rearrange("p (r t) -> p r t", r=2)
        sp_a = shared[:, 6 * GT:7 * GT]
        sp_e = shared[:, 7 * GT:8 * GT]
        bc = sb("bc", [P, T], BF16)
        bc_rest = sb("bc_rest", [P, GT])
        rings = staging[:].rearrange("p a b -> p (a b)")[:, 0:6 * GT].rearrange("p (w r t) -> p w r t", w=3, r=2)
        c_row, bx, hs = rings[:, 0], rings[:, 1], rings[:, 2]

        consts_in_s, vectors_in_s, mats_in_s = sem("consts_loaded"), sem("vectors_loaded"), sem("mats_loaded")
        x_loaded = [sem(f"x_loaded_{g}") for g in range(GROUPS)]
        w_loaded = [sem(f"w_loaded_{i}") for i in range(2)]
        w_hi_done, w_lo_done = sem("w_hi_done"), sem("w_lo_done")
        dve_order, act_order, pool_order = sem("dve_order"), sem("act_order"), sem("pool_order")
        consts_ready = sem("consts_ready")
        setup_mm, setup_copied = sem("setup_mm"), sem("setup_copied")
        xnT_padded = sem("xnT_padded")
        var_ready, rstd0_ready, xn_ready = sem("var_ready"), sem("rstd0_ready"), sem("xn_ready")
        xn_turned, xnT_ready = sem("xn_turned"), sem("xnT_ready")
        xn_stored = [sem(f"xn_stored_{g}") for g in range(GROUPS)]
        logits_ready, ldiff_ready, e2_ready = sem("logits_ready"), sem("ldiff_ready"), sem("e2_ready")
        picked_ready, prefix_ready = sem("picked_ready"), sem("prefix_ready")
        onehot_ready, onehot_used = sem("onehot_ready"), sem("onehot_used")
        ids_ready, index_ready = sem("ids_ready"), sem("index_ready")
        gathered = [sem(f"gathered_{r}") for r in range(RING)]
        scattered = [sem(f"scattered_{r}") for r in range(RING)]
        x_turned, xT_hi_done, xT_ready = sem("x_turned"), sem("xT_hi_done"), sem("xT_ready")
        gate_done, gelu_done = sem("gate_done"), sem("gelu_done")
        up_done, hact_done = sem("up_done"), sem("hact_done")
        h_turned, hT_hi_done, hT_ready = sem("h_turned"), sem("hT_hi_done"), sem("hT_ready")
        down_done, y_ready = sem("down_done"), sem("y_ready")
        y_loaded = [sem(f"y_loaded_{i}") for i in range(3)]
        x_moved = sem("x_moved")
        xz_done, silu_done, gate_ready = sem("xz_done"), sem("silu_done"), sem("gate_ready")
        proj_done, abs_done, exp_done, log_done = sem("proj_done"), sem("abs_done"), sem("exp_done"), sem("log_done")
        dg_ready, bc_hi_done, bc_rest_done, bc_mid_done, bc_ready = (
            sem("dg_ready"), sem("bc_hi_done"), sem("bc_rest_done"), sem("bc_mid_done"), sem("bc_ready"))
        cb_added = sem("cb_added")
        b_spread, c_spread, c_copied, decay_ready = sem("b_spread"), sem("c_spread"), sem("c_copied"), sem("decay_ready")
        bx_ready, h_ready, hc_ready, hc_summed = sem("bx_ready"), sem("h_ready"), sem("hc_ready"), sem("hc_summed")
        yT_ready, y_turned, out_done, out_added = sem("yT_ready"), sem("y_turned"), sem("out_done"), sem("out_added")
        yvar_ready, yrstd0_ready = sem("yvar_ready"), sem("yrstd0_ready")
        stored = sem("stored")

        def spread(ap, axis, shape):
            return ap.unsqueeze(axis).to_broadcast(shape)

        def batch_pair(q):
            return xnT[:, 2 * q:2 * q + 2, PAD:BLEN]

        def grp(g):
            return slice(g * GC, (g + 1) * GC)

        block = ctx.enter_context(nc.Block())

        @block.sync
        def _(sp):
            for g in range(GROUPS):
                sp.dma_start(x[:, grp(g), :], x_in[:, grp(g), :]).then_inc(x_loaded[g], 16)
                if g == 0:
                    sp.dma_start(consts[:], consts_in).then_inc(consts_in_s, 16)
            sp.dma_start(mats[:], mats_in).then_inc(mats_in_s, 16)
            sp.dma_start(vectors[:], vectors_in).then_inc(vectors_in_s, 16)
            for e in range(E):
                if e >= 2:
                    sp.wait_ge(w_hi_done, e - 1)
                    sp.wait_ge(w_lo_done, e - 1)
                sp.dma_start(staging[:, e % 2, :], experts_in[:, e, :]).then_inc(w_loaded[e % 2], 16)

            for l in range(2):
                rows = xn_dram[l].rearrange("(c p) d -> p c d", p=P)
                y_rows = y_dram[l].rearrange("(k c p) d -> p k c d", k=TOPK, p=P)
                for g in range(GROUPS):
                    sp.wait_ge(xn_ready, 2 * l * GROUPS + g + 1)
                    sp.dma_start(rows[:, grp(g), :], xn[:, grp(g), :]).then_inc(xn_stored[g], 16)
                for r in range(RING):
                    sp.wait_ge(scattered[r], 16 * (l + 1) * (NT // RING))
                for g in range(GROUPS):
                    if l or g == 3:
                        sp.wait_ge(x_moved, l * GROUPS + g - 2)
                    for k in range(TOPK):
                        sp.dma_start(ybuf[:, g % 3, k], y_rows[:, k, grp(g), :]).then_inc(y_loaded[g % 3], 16)
            for g in range(GROUPS):
                sp.wait_ge(x_moved, GROUPS + g + 1)
                sp.dma_start(out[:, grp(g), :], x[:, grp(g), :]).then_inc(stored, 16)
            sp.wait_ge(stored, 16 * GROUPS)

        @block.gpsimd
        def _(pool):
            order = [0]

            def chain(ins):
                order[0] += 1
                ins.then_inc(pool_order, 1)
                pool.wait_ge(pool_order, order[0])

            pool.memset(ones_b[:], 1.0)
            pool.memset(ones_f[:], 1.0)
            pool.memset(picked[:, C, :], 0.0)
            pool.memset(xnT[:, :, 0:PAD], 0.0).then_inc(xnT_padded, 1)
            for e in range(E):
                pool.wait_ge(w_hi_done, e + 1)
                pool.tensor_tensor(w_lo[:, e, :], staging[:, e % 2, :], w_hi[:, e, :].bitcast(F32),
                                   ALU.subtract).then_inc(w_lo_done, 1)

            def ffn(l):
                t0 = l * NT

                def get(t):
                    r = t % RING
                    if t >= RING:
                        pool.wait_ge(x_turned, t0 + t - RING + 1)
                    pool.indirect_dma_start(
                        out=xg[:, r, :], out_offset=None, in_=xn_dram[l],
                        in_offset=bass.IndirectOffsetOnAxis(ap=get_i[:, t:t + 1].bitcast(U32), axis=0),
                        bounds_check=T - 1, oob_is_err=False).then_inc(gathered[r], 16)

                def put(t):
                    pool.wait_ge(y_ready, t0 + t + 1)
                    pool.indirect_dma_start(
                        out=y_dram[l], in_=ysb[:, t % RING, :], in_offset=None,
                        out_offset=bass.IndirectOffsetOnAxis(ap=put_i[:, t:t + 1].bitcast(U32), axis=0),
                        bounds_check=TOPK * T - 1, oob_is_err=False).then_inc(scattered[t % RING], 16)

                pool.wait_ge(index_ready, l + 1)
                for g in range(GROUPS):
                    pool.wait_ge(xn_stored[g], 16 * (l + 1))
                for t in range(RING):
                    get(t)
                for t in range(NT):
                    if t + RING < NT:
                        get(t + RING)
                    put(t)

            def mamba():
                pool.wait_ge(setup_copied, 3)
                pool.wait_ge(xn_ready, 2 * GROUPS)
                pool.tensor_tensor(x[:], x[:], spread(out_c[:], 1, [P, C, D]), ALU.add).then_inc(cb_added, 1)
                pool.wait_ge(cb_added, 1)
                for q in range(GROUPS):
                    cols = slice(q * GT, (q + 1) * GT)
                    pool.wait_ge(bc_rest_done, q + 1)
                    chain(pool.tensor_copy(bc[32:64, cols], bc_rest[32:64, :]))
                    pool.tensor_copy(bc[64:96, cols], bc_rest[64:96, :]).then_inc(bc_mid_done, 1)
                    pool.wait_ge(bc_mid_done, q + 1)
                    pool.tensor_tensor(bc[64:96, cols], bc_rest[64:96, :], bc[64:96, cols],
                                       ALU.subtract).then_inc(bc_ready, 1)
                    pool.wait_ge(bc_ready, q + 1)

                def step(k, n, ring_new):
                    pool.wait_ge(h_ready, k + 1)
                    pool.wait_ge(c_copied, k + 1)
                    if not ring_new:
                        pool.wait_ge(hc_summed, k - 3)
                    pool.tensor_tensor(hc[:, n % 4, :], hs[:, n % 2, :], c_row[:, n % 2, :],
                                       ALU.mult).then_inc(hc_ready, 1)

                for n in range(N):
                    step(n, n, n < 4)
                with pool.Fori(1, GROUPS) as q:
                    for n in range(N):
                        step(q * N + n, n, False)

            ffn(0)
            mamba()
            ffn(1)

        @block.scalar
        def _(act):
            def normalise(s):
                for g in range(GROUPS):
                    v = slice(g * GC, (g + 1) * GC)
                    act.wait_ge(var_ready, s * GROUPS + g + 1)
                    nc.scalar.activation(ln_v[:, v], var_e[:, v], ACT.Ln).then_inc(act_order, 1)
                    order[0] += 1
                    act.wait_ge(act_order, order[0])
                    nc.scalar.activation(rstd0[:, v], ln_v[:, v], ACT.Exp, scale=-0.5).then_inc(rstd0_ready, 1)
                    if g >= 1:
                        copy_turned(s, g - 1)
                copy_turned(s, GROUPS - 1)

            def copy_turned(s, g):
                act.wait_ge(xn_turned, s * GROUPS + g + 1)
                nc.scalar.copy(batch_pair(g), ps[:, LNB[s] + g % 2, :].rearrange("p (b t) -> p b t", b=2)
                               ).then_inc(xnT_ready, 1)

            order = [0]
            LNB = (0, 4, 4)

            def split_weights(e):
                act.wait_ge(w_loaded[e % 2], 16 * (e // 2 + 1))
                nc.scalar.copy(w_hi[:, e, :], staging[:, e % 2, :]).then_inc(w_hi_done, 1)

            def ffn(l):
                t0 = l * NT
                act.wait_ge(ldiff_ready, l + 1)
                nc.scalar.activation(e2[:], ldiff[:], ACT.Exp).then_inc(e2_ready, 1)

                def x_hi(t, r, first):
                    act.wait_ge(x_turned, t0 + t + 1)
                    if not first:
                        act.wait_ge(up_done, t0 + t - RING + 1)
                    nc.scalar.copy(xT_hi[:, r, :], ps[:, 0, 0:P]).then_inc(xT_hi_done, 1)

                def act_gelu(t, first):
                    act.wait_ge(gate_done, t0 + t + 1)
                    if not first:
                        act.wait_ge(hact_done, t0 + t)
                    nc.scalar.activation(gelu[:], ps[:, 1, :], ACT.Gelu).then_inc(gelu_done, 1)

                def h_hi(t, first):
                    act.wait_ge(h_turned, t0 + t + 1)
                    if not first:
                        act.wait_ge(down_done, t0 + t)
                    nc.scalar.copy(hT_hi[:], ps[:, 3, :]).then_inc(hT_hi_done, 1)

                def y_out(t, r, n, first):
                    act.wait_ge(down_done, t0 + t + 1)
                    if not first:
                        act.wait_ge(scattered[r], (l * (NT // RING) + n) * 16)
                    nc.scalar.copy(ysb[:, r, :], ps[:, 4, 0:D]).then_inc(y_ready, 1)

                x_hi(0, 0, l == 0)
                act_gelu(0, l == 0)
                x_hi(1, 1, l == 0)

                def step(i, u, n, cold, last=False):
                    h_hi(i - 1, cold and u == 0)
                    act_gelu(i, False)
                    if not last:
                        x_hi(i + 1, (u + 2) % RING, cold and u == 0)
                    y_out(i - 1, u, n, cold)

                for u in range(RING):
                    step(1 + u, u, 0, l == 0)
                with act.Fori(1, LOOPS) as m:
                    for u in range(RING):
                        step(m * RING + (1 + u), u, m, False)
                step(NT - 2, 0, LOOPS, False)
                step(NT - 1, 1, LOOPS, False, last=True)
                h_hi(NT - 1, False)
                y_out(NT - 1, 2, LOOPS, False)

            def mamba():
                for q in range(GROUPS):
                    act.wait_ge(xz_done, q + 1)
                    if q >= 2:
                        act.wait_ge(gate_ready, q - 1)
                    nc.scalar.activation(silu[:, q % 2, :], ps[:, q % 2, :], ACT.Silu,
                                         bias=vectors[:, V_BCONV:V_BCONV + 1]).then_inc(silu_done, 1)
                for q in range(GROUPS):
                    act.wait_ge(proj_done, q + 1)
                    if q >= 1:
                        act.wait_ge(dg_ready, q)
                    nc.scalar.activation(sp_a[:], ps[:, 4 + q % 2, :], ACT.Abs,
                                         bias=vectors[:, V_BDT:V_BDT + 1]).then_inc(abs_done, 1)
                    nc.scalar.copy(bc[0:BCR, q * GT:(q + 1) * GT], ps[0:BCR, 6 + q % 2, :]).then_inc(bc_hi_done, 1)
                    act.wait_ge(abs_done, q + 1)
                    nc.scalar.activation(sp_e[:], sp_a[:], ACT.Exp, scale=-1.0).then_inc(exp_done, 1)
                    act.wait_ge(exp_done, q + 1)
                    nc.scalar.activation(sp_a[:], sp_e[:], ACT.Ln, bias=1.0).then_inc(log_done, 1)

                def step(q, n, first):
                    k = q * N + n
                    if not first:
                        act.wait_ge(h_ready, k - 1)
                        act.wait_ge(hc_ready, k - 1)
                    act.wait_ge(c_spread, k + 1)
                    nc.scalar.copy(c_row[:, n % 2, :], ps[:, 2 + n % 2, :]).then_inc(c_copied, 1)
                    nc.scalar.activation(ps[:, 4 + n % 2, :], delta[:, bass.ds(q * GT, GT)], ACT.Exp,
                                         scale=neg_a[:, n:n + 1]).then_inc(decay_ready, 1)

                act.wait_ge(dg_ready, GROUPS)
                for n in range(N):
                    step(0, n, n < 2)
                with act.Fori(1, GROUPS) as q:
                    for n in range(N):
                        step(q, n, False)

                for q in range(GROUPS):
                    v = slice(q * GC, (q + 1) * GC)
                    act.wait_ge(yvar_ready, q + 1)
                    nc.scalar.activation(ln_v[:, v], var_e[:, v], ACT.Ln).then_inc(act_order, 1)
                    order[0] += 1
                    act.wait_ge(act_order, order[0])
                    nc.scalar.activation(rstd0[:, v], ln_v[:, v], ACT.Exp, scale=-0.5).then_inc(yrstd0_ready, 1)

            split_weights(0)
            split_weights(1)
            normalise(0)
            for e in range(2, E):
                split_weights(e)
            act.wait_ge(setup_mm, 1)
            nc.scalar.copy(conv_w[:].rearrange("p a b -> p (a b)"), ps[:, 5, :]).then_inc(setup_copied, 1)
            act.wait_ge(setup_mm, 2)
            nc.scalar.copy(out_w[:], ps[:, 6, 0:P]).then_inc(setup_copied, 1)
            nc.scalar.activation(neg_a[:], vectors[:, V_ALOG:V_ALOG + N], ACT.Exp).then_inc(act_order, 1)
            order[0] += 1
            act.wait_ge(act_order, order[0])
            nc.scalar.mul(neg_a[:], neg_a[:], -1.0).then_inc(act_order, 1)
            order[0] += 1
            act.wait_ge(act_order, order[0])
            ffn(0)
            normalise(1)
            mamba()
            normalise(2)
            ffn(1)

        @block.tensor
        def _(pe):
            LNB = (0, 4, 4)

            def turn_group(s):
                for g in range(GROUPS):
                    pe.wait_ge(xn_ready, s * GROUPS + g + 1)
                    if g >= 2:
                        pe.wait_ge(xnT_ready, s * GROUPS + g - 1)
                    for c in range(GC):
                        t = pe.transpose(ps[:, LNB[s] + g % 2, c * P:(c + 1) * P], xn[:, g * GC + c, :], ident)
                    t.then_inc(xn_turned, 1)

            def split_product(acc, x_hi, x_lo, w_cols, first, last):
                pe.matmul(acc, x_hi, w_hi[:].rearrange("p e w -> p (e w)")[:, w_cols], start=first, stop=False)
                pe.matmul(acc, x_hi, w_lo[:].rearrange("p e w -> p (e w)")[:, w_cols], start=False, stop=False)
                return pe.matmul(acc, x_lo, w_hi[:].rearrange("p e w -> p (e w)")[:, w_cols], start=False, stop=last)

            def route(l):
                for g in range(GROUPS):
                    pe.wait_ge(xnT_ready, 2 * l * GROUPS + g + 1)
                    for c in range(GC):
                        at = 2 * g + c // 2, PAD + (c % 2) * P
                        m = pe.matmul(ps[:, 2, (g * GC + c) * E:(g * GC + c + 1) * E],
                                      xnT[:, at[0], at[1]:at[1] + P], mats[:, M_GATE:M_GATE + E],
                                      start=True, stop=True)
                m.then_inc(logits_ready, 1)
                pe.wait_ge(picked_ready, l + 1)
                flat = picked[:].rearrange("p c e -> p (c e)")
                w = (C + 1) * E
                pe.matmul(ps[:, 3, 0:w], tri_b[:], flat, start=True, stop=False)
                for s in range(1, C + 1):
                    m = pe.matmul(ps[:, 3, s * E:w], ones_b[:], flat[:, 0:w - s * E], start=False, stop=(s == C))
                m.then_inc(prefix_ready, 1)
                for g in range(GROUPS):
                    pe.wait_ge(onehot_ready, l * GROUPS + g + 1)
                    for i in range(JP):
                        j = g * JP + i
                        m = pe.matmul(ps[:, 4, 0:2 * NT], in_row[:, g % 2, i, :],
                                      ids_rhs[:, j].rearrange("p v t -> p (v t)"), start=(j == 0), stop=(j == J - 1))
                    m.then_inc(onehot_used, 1)

            def ffn(l):
                t0 = l * NT

                def turn_x(t, r, n):
                    pe.wait_ge(gathered[r], (l * (NT // RING) + n + 1) * 16)
                    pe.wait_ge(xT_ready, t0 + t)
                    pe.transpose(ps[:, 0, 0:P], xg[:, r, :], ident).then_inc(x_turned, 1)

                def gate_p(t, r, w0):
                    pe.wait_ge(xT_ready, t0 + t + 1)
                    pe.wait_ge(gelu_done, t0 + t)
                    split_product(ps[:, 1, :], xT_hi[:, r, :], xT_lo[:, r, :], bass.ds(w0, F),
                                  True, True).then_inc(gate_done, 1)

                def up_p(t, r, w0):
                    pe.wait_ge(hact_done, t0 + t)
                    split_product(ps[:, 2, :], xT_hi[:, r, :], xT_lo[:, r, :], bass.ds(w0 + F, F),
                                  True, True).then_inc(up_done, 1)

                def turn_h(t):
                    pe.wait_ge(hact_done, t0 + t + 1)
                    pe.wait_ge(hT_ready, t0 + t)
                    for f in range(FC):
                        m = pe.transpose(ps[:, 3, f * P:(f + 1) * P], hact[:, f * P:(f + 1) * P], ident)
                    m.then_inc(h_turned, 1)

                def down_p(t, w0):
                    pe.wait_ge(hT_ready, t0 + t + 1)
                    pe.wait_ge(y_ready, t0 + t)
                    for f in range(FC):
                        m = split_product(ps[:, 4, 0:D], hT_hi[:, f * P:(f + 1) * P], hT_lo[:, f * P:(f + 1) * P],
                                          bass.ds(w0 + (2 * F + f * D), D), f == 0, f == FC - 1)
                    m.then_inc(down_done, 1)

                def weights_of(t):
                    return pe.value_load(exp_i[0:1, bass.ds(t, 1)], min_val=0, max_val=E - 1) * WCOLS

                pe.wait_ge(index_ready, l + 1)
                pe.wait_ge(w_lo_done, E)
                w0 = weights_of(0)
                turn_x(0, 0, 0)
                gate_p(0, 0, w0)
                up_p(0, 0, w0)
                turn_x(1, 1, 0)

                def step(i, u, n_next, last=False):
                    before, w = weights_of(i - 1), weights_of(i)
                    turn_h(i - 1)
                    gate_p(i, (u + 1) % RING, w)
                    up_p(i, (u + 1) % RING, w)
                    if not last:
                        turn_x(i + 1, (u + 2) % RING, n_next)
                    down_p(i - 1, before)

                with pe.Fori(0, LOOPS) as m:
                    for u in range(RING):
                        step(m * RING + (1 + u), u, m + (u + 2) // RING)
                step(NT - 2, 0, LOOPS)
                step(NT - 1, 1, 0, last=True)
                turn_h(NT - 1)
                down_p(NT - 1, weights_of(NT - 1))

            def mamba():
                for q in range(GROUPS):
                    if q >= 2:
                        pe.wait_ge(gate_ready, q - 1)
                    pe.wait_ge(xnT_ready, GROUPS + q + 1)
                    for k in range(TAPS):
                        pe.matmul(ps[:, q % 2, :], conv_w[:, k, :], xnT[:, 2 * q:2 * q + 2, PAD - TAPS + 1 + k:PAD - TAPS + 1 + k + L],
                                  start=(k == 0), stop=(k == TAPS - 1))
                    pe.matmul(ps[:, 2 + q % 2, :], mats[:, M_INZ:M_INZ + D], batch_pair(q),
                              start=True, stop=True).then_inc(xz_done, 1)
                for q in range(GROUPS):
                    cols = slice(q * GT, (q + 1) * GT)
                    pe.wait_ge(gate_ready, q + 1)
                    if q >= 2:
                        pe.wait_ge(dg_ready, q - 1)
                        pe.wait_ge(bc_rest_done, q - 1)
                    pe.matmul(ps[:, 4 + q % 2, :], mats[:, M_DT:M_DT + D], gate[:, cols], start=True, stop=True)
                    pe.matmul(ps[0:BCR, 6 + q % 2, :], mats[:, M_BC:M_BC + BCR], gate[:, cols],
                              start=True, stop=True).then_inc(proj_done, 1)

                def spread_bc(q, n, first):
                    k = q * N + n
                    if not first:
                        pe.wait_ge(bx_ready, k - 1)
                    pe.matmul(ps[:, n % 2, :], sel_b[0:BCR, n:n + 1].to_broadcast([BCR, P]),
                              bc[0:BCR, bass.ds(q * GT, GT)], start=True, stop=True).then_inc(b_spread, 1)
                    if not first:
                        pe.wait_ge(c_copied, k - 1)
                    pe.matmul(ps[:, 2 + n % 2, :], sel_b[0:BCR, N + n:N + n + 1].to_broadcast([BCR, P]),
                              bc[0:BCR, bass.ds(q * GT, GT)], start=True, stop=True).then_inc(c_spread, 1)

                def sum_states(q, n, first):
                    k = q * N + n
                    pe.wait_ge(hc_ready, k + 1)
                    if n == 0 and not first:
                        pe.wait_ge(yT_ready, q)
                    pe.matmul(ps[:, 6, :], ident, hc[:, n % 4, :], start=(n == 0), stop=(n == N - 1)
                              ).then_inc(hc_summed, 1)

                pe.wait_ge(bc_ready, GROUPS)
                for n in range(LAG):
                    spread_bc(0, n, n < 2)
                for n in range(N):
                    sum_states(0, n, True)
                    spread_bc((n + LAG) // N, (n + LAG) % N, False)
                with pe.Fori(1, GROUPS - 1) as q:
                    for n in range(N):
                        sum_states(q, n, False)
                        spread_bc(q + (n + LAG) // N, (n + LAG) % N, False)
                for n in range(N):
                    sum_states(GROUPS - 1, n, False)
                    if n + LAG < N:
                        spread_bc(GROUPS - 1, n + LAG, False)

                for q in range(GROUPS):
                    pe.wait_ge(yT_ready, q + 1)
                    if q >= 2:
                        pe.wait_ge(out_added, q - 1)
                    for c in range(GC):
                        m = pe.transpose(ps[:, q % 2, c * P:(c + 1) * P], xnT[:, 2 * q + c // 2, PAD + (c % 2) * P:PAD + (c % 2) * P + P], ident)
                    m.then_inc(y_turned, 1)
                    for c in range(GC):
                        m = pe.matmul(ps[:, 2 + q % 2, c * P:(c + 1) * P], xnT[:, 2 * q + c // 2, PAD + (c % 2) * P:PAD + (c % 2) * P + P],
                                      out_w[:], start=True, stop=True)
                    m.then_inc(out_done, 1)

            pe.wait_ge(consts_in_s, 16)
            turn_group(0)
            pe.wait_ge(mats_in_s, 16)
            pe.wait_ge(consts_ready, 1)
            for k in range(TAPS):
                m = pe.transpose(ps[:, 5, k * P:(k + 1) * P], conv_rows[:, k, :], ident)
            m.then_inc(setup_mm, 1)
            pe.matmul(ps[:, 6, 0:P], consts[:, K_CENTRE:K_CENTRE + P], out_g[:], start=True, stop=True).then_inc(setup_mm, 1)
            pe.matmul(ps[:, 7, 0:P], beta_b[:], mats[:, M_OUT:M_OUT + D], start=True, stop=True).then_inc(setup_mm, 1)
            route(0)
            ffn(0)
            turn_group(1)
            mamba()
            turn_group(2)
            route(1)
            ffn(1)

        @block.vector
        def _(dve):
            order = [0]

            def chain(ins):
                order[0] += 1
                ins.then_inc(dve_order, 1)
                dve.wait_ge(dve_order, order[0])

            def refine(v, ready_sem, value):
                dve.wait_ge(ready_sem, value)
                chain(dve.tensor_tensor(nt0[:, v], var_e[:, v], rstd0[:, v], ALU.mult))
                chain(dve.tensor_tensor(nt1[:, v], nt0[:, v], rstd0[:, v], ALU.mult))
                chain(dve.tensor_scalar(nt0[:, v], nt1[:, v], -0.5, 1.5, ALU.mult, ALU.add))
                chain(dve.tensor_tensor(rstd[:, v], nt0[:, v], rstd0[:, v], ALU.mult))

            def statistics(rows, g, ready_sem):
                for c in range(GC):
                    i = dve.bn_stats(stats[:, g * GC + c, :], rows(c))
                chain(i)
                for c in range(GC):
                    i = dve.bn_aggr(mv[:, g * GC + c, :], stats[:, g * GC + c, :])
                chain(i)
                dve.tensor_scalar(var_e[:, grp(g)], mv[:, grp(g), 1], EPS, None, ALU.add).then_inc(ready_sem, 1)

            def normalise(s, arrive):
                for g in range(GROUPS + 1):
                    if g < GROUPS:
                        arrive(g)
                        statistics(lambda c: x[:, g * GC + c, :], g, var_ready)
                    if g >= 1:
                        h = g - 1
                        refine(grp(h), rstd0_ready, s * GROUPS + h + 1)
                        if s:
                            dve.wait_ge(xn_stored[h], 16)
                        for c in range(h * GC, (h + 1) * GC):
                            i = dve.tensor_scalar(xn[:, c, :], x[:, c, :], mv[:, c, 0:1], rstd[:, c:c + 1],
                                                  ALU.subtract, ALU.mult)
                        i.then_inc(xn_ready, 1)

            def route(l):
                dve.wait_ge(logits_ready, l + 1)
                chain(dve.tensor_copy(lg[:].rearrange("p c e -> p (c e)"), ps[:, 2, 0:C * E]))
                dve.memset(shared[:, 0:C * E * E].rearrange("p (c o) -> p c o", c=C)[:, :, 0:E * E:E + 1], 0.0)
                for e in range(E):
                    if e:
                        i = dve.tensor_tensor(beats[:, :, e, 0:e], lg[:, :, 0:e],
                                              lg[:, :, e:e + 1].to_broadcast([P, C, e]), ALU.is_ge)
                    if e < E - 1:
                        i = dve.tensor_tensor(beats[:, :, e, e + 1:E], lg[:, :, e + 1:E],
                                              lg[:, :, e:e + 1].to_broadcast([P, C, E - 1 - e]), ALU.is_gt)
                chain(i)
                chain(dve.tensor_reduce(rank[:], beats[:], AX.X, ALU.add))
                dve.tensor_scalar(picked[:, 0:C, :], rank[:], 2.0, None, ALU.is_lt).then_inc(picked_ready, 1)
                dve.tensor_scalar(top[:, 0], rank[:], 0.0, None, ALU.is_equal)
                chain(dve.tensor_scalar(top[:, 1], rank[:], 1.0, None, ALU.is_equal))
                chain(dve.tensor_tensor(prod[:], top[:], spread(lg[:], 1, [P, TOPK, C, E]), ALU.mult))
                chain(dve.tensor_reduce(lsel[:], prod[:], AX.X, ALU.add))
                dve.tensor_tensor(ldiff[:], lsel[:, 1], lsel[:, 0], ALU.subtract).then_inc(ldiff_ready, 1)

                dve.wait_ge(prefix_ready, l + 1)
                counts = ps[:, 3, C * E:(C + 1) * E]
                chain(dve.tensor_tensor(over[:], spread(counts, 2, [P, E, C]),
                                        spread(consts[:, K_TILE:K_TILE + C], 1, [P, E, C]), ALU.is_gt))
                chain(dve.tensor_reduce(ntile[:], over[:], AX.X, ALU.add))
                chain(dve.tensor_tensor_scan(tile_end[:], ones_f[:], ntile[:], 0.0, ALU.mult, ALU.add))
                chain(dve.tensor_tensor(base[:], tile_end[:], ntile[:], ALU.subtract))
                chain(dve.tensor_scalar(base[:], base[:], float(P), None, ALU.mult))
                chain(dve.tensor_tensor(slot[:], ps[:, 3, 0:C * E].rearrange("p (c e) -> p c e", e=E),
                                        spread(base[:], 1, [P, C, E]), ALU.add))
                chain(dve.tensor_tensor(prod[:], top[:], spread(slot[:], 1, [P, TOPK, C, E]), ALU.mult))
                chain(dve.tensor_reduce(slot_f[:].rearrange("p (k c) -> p k c", k=TOPK), prod[:], AX.X, ALU.add))
                chain(dve.tensor_copy(slot_i[:], slot_f[:]))
                dve.tensor_scalar(tile_i[:], slot_i[:], P.bit_length() - 1, None, ALU.arith_shift_right)
                chain(dve.tensor_scalar(row_i[:], slot_i[:], P - 1, None, ALU.bitwise_and))
                dve.tensor_copy(tile_f[:], tile_i[:])
                chain(dve.tensor_copy(row_f[:], row_i[:]))
                iota = consts[:, K_IOTA:K_IOTA + P]
                chain(dve.tensor_tensor(in_tile[:], spread(iota[:, 0:NT], 1, [P, J, NT]),
                                        spread(tile_f[:], 2, [P, J, NT]), ALU.is_equal))
                dve.tensor_tensor(ids_rhs[:, :, 0, :], in_tile[:],
                                  spread(consts[:, K_JP1:K_JP1 + J], 2, [P, J, NT]), ALU.mult)
                dve.tensor_scalar(ids_rhs[:, :, 1, :], in_tile[:], consts[:, K_P:K_P + 1], None, ALU.mult)
                for g in range(GROUPS):
                    if l or g >= 2:
                        dve.wait_ge(onehot_used, l * GROUPS + g - 1)
                    dve.tensor_tensor(in_row[:, g % 2], spread(iota, 1, [P, JP, P]),
                                      spread(row_f[:, g * JP:(g + 1) * JP], 2, [P, JP, P]),
                                      ALU.is_equal).then_inc(onehot_ready, 1)
                chain(dve.tensor_tensor(le_end[:], spread(iota[:, 0:NT], 2, [P, NT, E]),
                                        spread(tile_end[:], 1, [P, NT, E]), ALU.is_ge))
                chain(dve.tensor_reduce(exp_f[:], le_end[:], AX.X, ALU.add))
                dve.tensor_scalar(exp_i[:], exp_f[:], float(E - 1), None, ALU.min)
                dve.wait_ge(e2_ready, l + 1)
                chain(dve.tensor_scalar(den[:], e2[:], 1.0, None, ALU.add))
                chain(dve.reciprocal(den[:], den[:]))
                dve.tensor_scalar(half_w[:, 0], den[:], 0.5, None, ALU.mult)
                chain(dve.tensor_tensor(half_w[:, 1], den[:], e2[:], ALU.mult))
                chain(dve.tensor_scalar(half_w[:, 1], half_w[:, 1], 0.5, None, ALU.mult))
                dve.wait_ge(onehot_used, (l + 1) * GROUPS)
                chain(dve.tensor_copy(ids[:].rearrange("p v t -> p (v t)"), ps[:, 4, 0:2 * NT]))
                chain(dve.scalar_tensor_tensor(out=id128[:], in0=ids[:, 0], scalar=float(P), in1=ids[:, 1],
                                               op0=ALU.mult, op1=ALU.add))
                chain(dve.tensor_scalar(empty[:], id128[:], 1.0, float(TOPK * T + P), ALU.is_lt, ALU.mult))
                chain(dve.scalar_tensor_tensor(out=put_i[:], in0=empty[:], scalar=-float(P), in1=id128[:],
                                               op0=ALU.add, op1=ALU.add))
                dve.tensor_scalar(get_i[:], put_i[:], T - 1, None, ALU.bitwise_and).then_inc(index_ready, 1)

            def ffn(l):
                t0 = l * NT

                def x_lo(t, r, first):
                    dve.wait_ge(xT_hi_done, t0 + t + 1)
                    if not first:
                        dve.wait_ge(up_done, t0 + t - RING + 1)
                    dve.tensor_tensor(xT_lo[:, r, :], ps[:, 0, 0:P], xT_hi[:, r, :].bitcast(F32),
                                      ALU.subtract).then_inc(xT_ready, 1)

                def h_act(t, first):
                    dve.wait_ge(up_done, t0 + t + 1)
                    dve.wait_ge(gelu_done, t0 + t + 1)
                    if not first:
                        dve.wait_ge(h_turned, t0 + t)
                    dve.tensor_tensor(hact[:], ps[:, 2, :], gelu[:], ALU.mult).then_inc(hact_done, 1)

                def h_lo(t, first):
                    dve.wait_ge(hT_hi_done, t0 + t + 1)
                    if not first:
                        dve.wait_ge(down_done, t0 + t)
                    dve.tensor_tensor(hT_lo[:], ps[:, 3, :], hT_hi[:].bitcast(F32),
                                      ALU.subtract).then_inc(hT_ready, 1)

                x_lo(0, 0, l == 0)
                h_act(0, l == 0)
                x_lo(1, 1, l == 0)

                def step(i, u, cold, last=False):
                    h_lo(i - 1, cold and u == 0)
                    h_act(i, False)
                    if not last:
                        x_lo(i + 1, (u + 2) % RING, cold and u == 0)

                for u in range(RING):
                    step(1 + u, u, l == 0)
                with dve.Fori(1, LOOPS) as m:
                    for u in range(RING):
                        step(m * RING + (1 + u), u, False)
                step(NT - 2, 0, False)
                step(NT - 1, 1, False, last=True)
                h_lo(NT - 1, False)

            def add_experts(l, g):
                loads = sum(1 for i in range(l * GROUPS + g + 1) if i % GROUPS % 3 == g % 3)
                dve.wait_ge(y_loaded[g % 3], 16 * TOPK * loads)
                for k in range(TOPK):
                    for c in range(GC):
                        at = g * GC + c
                        i = dve.scalar_tensor_tensor(out=x[:, at, :], in0=ybuf[:, g % 3, k, c, :],
                                                     scalar=half_w[:, k, at:at + 1], in1=x[:, at, :],
                                                     op0=ALU.mult, op1=ALU.add)
                    if k == 0:
                        chain(i)
                i.then_inc(x_moved, 1)
                dve.wait_ge(x_moved, l * GROUPS + g + 1)

            def mamba():
                for q in range(GROUPS):
                    dve.wait_ge(silu_done, q + 1)
                    dve.tensor_tensor(gate[:, q * GT:(q + 1) * GT], ps[:, 2 + q % 2, :], silu[:, q % 2, :],
                                      ALU.mult).then_inc(gate_ready, 1)
                for q in range(GROUPS):
                    cols = slice(q * GT, (q + 1) * GT)
                    dve.wait_ge(bc_hi_done, q + 1)
                    if q:
                        dve.wait_ge(bc_ready, q)
                    dve.tensor_tensor(bc_rest[32:64, :], ps[32:64, 6 + q % 2, :], bc[32:64, cols], ALU.subtract)
                    dve.tensor_tensor(bc_rest[64:96, :], ps[64:96, 6 + q % 2, :], bc[64:96, cols],
                                      ALU.subtract).then_inc(bc_rest_done, 1)
                    dve.wait_ge(abs_done, q + 1)
                    chain(dve.tensor_scalar(delta[:, cols], ps[:, 4 + q % 2, :], vectors[:, V_BDT:V_BDT + 1], 0.0,
                                            ALU.add, ALU.max))
                    dve.wait_ge(log_done, q + 1)
                    chain(dve.tensor_tensor(delta[:, cols], delta[:, cols], sp_a[:], ALU.add))
                    dve.tensor_tensor(gate[:, cols], gate[:, cols], delta[:, cols], ALU.mult).then_inc(dg_ready, 1)

                def y_add(q):
                    dve.wait_ge(hc_summed, (q + 1) * N)
                    at = xnT[:, bass.ds(q * 2, 2), PAD:BLEN]
                    dve.tensor_tensor(at, ps[:, 6, :].rearrange("p (b t) -> p b t", b=2), at,
                                      ALU.add).then_inc(yT_ready, 1)

                def step(q, n, first):
                    k = q * N + n
                    dve.wait_ge(b_spread, k + 1)
                    dve.tensor_tensor(bx[:, n % 2, :], ps[:, n % 2, :], gate[:, bass.ds(q * GT, GT)],
                                      ALU.mult).then_inc(bx_ready, 1)
                    dve.wait_ge(bx_ready, k + 1)
                    dve.wait_ge(decay_ready, k + 1)
                    if not first:
                        dve.wait_ge(hc_ready, k - 1)
                    for b in range(2):
                        t = slice(b * L, (b + 1) * L)
                        i = dve.tensor_tensor_scan(hs[:, n % 2, t], ps[:, 4 + n % 2, t], bx[:, n % 2, t], 0.0,
                                                   ALU.mult, ALU.add)
                    i.then_inc(h_ready, 1)

                dve.wait_ge(dg_ready, GROUPS)
                for n in range(N):
                    step(0, n, n < 2)
                with dve.Fori(1, GROUPS) as q:
                    for n in range(N):
                        step(q, n, False)
                        if n == 2:
                            y_add(q - 1)
                y_add(GROUPS - 1)
                dve.wait_ge(cb_added, 1)
                for q in range(GROUPS):
                    dve.wait_ge(y_turned, q + 1)
                    statistics(lambda c: ps[:, q % 2, c * P:(c + 1) * P], q, yvar_ready)
                    refine(grp(q), yrstd0_ready, q + 1)
                    dve.wait_ge(out_done, q + 1)
                    for c in range(GC):
                        at = q * GC + c
                        i = dve.scalar_tensor_tensor(out=x[:, at, :], in0=ps[:, 2 + q % 2, c * P:(c + 1) * P],
                                                     scalar=rstd[:, at:at + 1], in1=x[:, at, :],
                                                     op0=ALU.mult, op1=ALU.add)
                    i.then_inc(out_added, 1)

            dve.wait_ge(consts_in_s, 16)
            dve.tensor_copy(tri_b[:], consts[:, K_TRI:K_TRI + P])
            dve.tensor_copy(sel_b[:], consts[:, K_SEL:K_SEL + 2 * N])
            normalise(0, lambda g: dve.wait_ge(x_loaded[g], 16))
            dve.wait_ge(mats_in_s, 16)
            dve.wait_ge(vectors_in_s, 16)
            dve.wait_ge(xnT_padded, 1)
            for k in range(TAPS):
                dve.tensor_scalar(conv_rows[:, k, :], mats[:, M_INX:M_INX + D], vectors[:, V_CONV + k:V_CONV + k + 1],
                                  None, ALU.mult)
            dve.tensor_scalar(out_g[:], mats[:, M_OUT:M_OUT + D], vectors[:, V_GAMMA:V_GAMMA + 1], None, ALU.mult)
            dve.tensor_copy(beta_b[:], vectors[:, V_BETA:V_BETA + 1].to_broadcast([P, P])).then_inc(consts_ready, 1)
            route(0)
            dve.wait_ge(setup_mm, 3)
            dve.tensor_tensor(out_c[:], ps[:, 7, 0:P], mats[:, M_BOUT:M_BOUT + D], ALU.add).then_inc(setup_copied, 1)
            ffn(0)
            normalise(1, lambda g: add_experts(0, g))
            mamba()
            normalise(2, lambda g: dve.wait_ge(out_added, g + 1))
            route(1)
            ffn(1)
            for g in range(GROUPS):
                add_experts(1, g)


_INS = ["x_rows", "experts", "consts", "vectors", "mats"]


def _constants():
    import numpy as np

    k = np.zeros((P, K_COLS), np.float32)
    i = np.arange(P)
    k[:, K_IOTA:K_IOTA + P] = i
    k[:, K_TRI:K_TRI + P] = i[:, None] < i[None, :]
    k[:, K_CENTRE:K_CENTRE + P] = np.eye(P) - 1.0 / P
    k[:, K_IDENT:K_IDENT + P] = np.eye(P)
    k[:, K_TILE:K_TILE + C] = P * np.arange(C)
    k[:, K_JP1:K_JP1 + J] = np.arange(J) + 1
    k[:, K_P] = i
    k[:, K_SEL:K_SEL + 2 * N] = (i[:, None] % (2 * N)) == np.arange(2 * N)
    return k


def kernel(**inputs):
    import numpy as np
    import concourse.bacc as bacc
    from concourse.bass_utils import run_bass_kernel_spmd

    a = {k.split("_", 2)[2]: np.asarray(v) for k, v in inputs.items()}
    col = lambda v: v.reshape(P, -1)
    gu = a["gate_up_w"].transpose(2, 0, 1)
    dn = a["down_w"].reshape(E, D, FC, P).transpose(3, 0, 2, 1).reshape(P, E, FC * D)
    arrays = {
        "x_rows": a["x"].reshape(C, P, D).transpose(1, 0, 2),
        "experts": np.concatenate([gu, dn], axis=2),
        "consts": _constants(),
        "vectors": np.concatenate([col(a["b_conv"]), col(a["b_dt"]), col(a["ln_gamma"]), col(a["ln_beta"]),
                                   a["W_conv"].reshape(D, TAPS), a["A_log"]], axis=1),
        "mats": np.concatenate([a["W_in"][:D], a["W_in"][D:].T, a["W_dt"].T, a["W_out"].T,
                                np.broadcast_to(a["b_out"], (P, D))] + [a["W_xproj"].T] * BC_PARTS
                               + [a["gate_w"].T], axis=1),
    }
    arrays = {k: np.ascontiguousarray(v) for k, v in arrays.items()}
    nc = bacc.Bacc("TRN2", target_bir_lowering=False, num_devices=1)
    args = [nc.dram_tensor(f"in_{k}", arrays[k].shape, mybir.dt.from_np(arrays[k].dtype), kind="ExternalInput").ap()
            for k in _INS]
    args.append(nc.dram_tensor("out_rows", (P, C, D), F32, kind="ExternalOutput").ap())
    macaron_block(nc, *args)
    r = run_bass_kernel_spmd(nc, [{f"in_{k}": arrays[k] for k in _INS}], core_ids=[0])
    return r.results[0]["out_rows"].transpose(1, 0, 2).reshape(B, L, D)
```

```python
from contextlib import ExitStack

import concourse.bass as bass
from concourse import mybir

ALU = mybir.AluOpType
ACT = mybir.ActivationFunctionType
AX = mybir.AxisListType
F32 = mybir.dt.float32
F32R = mybir.dt.float32r
BF16 = mybir.dt.bfloat16
I32 = mybir.dt.int32
U32 = mybir.dt.uint32

P = 128
B, L, D = 8, 256, 128
T = B * L
C = T // P
GROUPS, GC = 4, C // 4
GT = GC * P
E, F, TOPK = 8, 512, 2
FC = F // P
J = TOPK * C
NT = (T * TOPK - E) // P + E
RING = 3
HEAD = 5
LOOPS = (NT - 1 - HEAD) // RING
GU = 2 * F
WCOLS = GU + FC * D
N = 16
TAPS = 4
PAD = TAPS
BLEN = L + PAD
EPS = 1e-5
BC_PARTS = 3
BCR = BC_PARTS * 2 * N
LAG = 4

K_IOTA, K_TRI, K_CENTRE, K_IDENT = 0, P, 2 * P, 3 * P
K_TILE = 4 * P
K_JP1 = K_TILE + C
K_P = K_JP1 + J
K_SEL = K_P + 1
K_COLS = K_SEL + 2 * N
V_BCONV, V_BDT, V_GAMMA, V_BETA, V_CONV = 0, 1, 2, 3, 4
V_ALOG = V_CONV + TAPS
V_COLS = V_ALOG + N
M_INX, M_INZ, M_DT, M_OUT, M_BOUT, M_BC = 0, D, 2 * D, 3 * D, 4 * D, 5 * D
M_GATE = M_BC + BCR
M_COLS = M_GATE + E

assert HEAD + LOOPS * RING == NT - 1


def past(value):
    return not isinstance(value, int) or value > 0


def tile_steps(engine, step):
    for i in range(1, HEAD):
        step(i, i % RING)
    with engine.Fori(0, LOOPS) as m:
        for u in range(RING):
            step(m * RING + (HEAD + u), (HEAD + u) % RING)
    step(NT - 1, (NT - 1) % RING)


def macaron_block(nc, x_in, experts_in, consts_in, vectors_in, mats_in, out):
    with ExitStack() as ctx:
        def sb(name, shape, dt=F32):
            return ctx.enter_context(nc.sbuf_tensor(name, shape, dt))

        def sem(name):
            return ctx.enter_context(nc.semaphore(name))

        xn_dram = [nc.dram_tensor(f"xn_rows_{l}", (T, D), F32).ap() for l in range(2)]
        y_dram = [nc.dram_tensor(f"expert_rows_{l}", (TOPK * T, D), F32).ap() for l in range(2)]

        ps = ctx.enter_context(nc.psum_tensor("ps", [P, 8, 512], F32))

        consts = sb("consts", [P, K_COLS])
        vectors = sb("vectors", [P, V_COLS])
        mats = sb("mats", [P, M_COLS])
        ident = consts[:, K_IDENT:K_IDENT + P]
        tri_b = sb("tri_b", [P, P], BF16)
        ones_b = sb("ones_b", [P, P], BF16)
        sel_b = sb("sel_b", [P, 2 * N], BF16)
        ones_f = sb("ones_f", [P, E])
        staging = sb("staging", [P, 2, WCOLS])
        w_hi = sb("w_hi", [P, E, GU], F32R)
        w_lo = sb("w_lo", [P, E, GU], F32R)
        w_down = sb("w_down", [P, E, FC, 2, D], F32R)
        neg_half = sb("neg_half", [P, C])
        conv_rows = sb("conv_rows", [P, TAPS, P])
        conv_w = sb("conv_w", [P, TAPS, P])
        out_g = sb("out_g", [P, P])
        out_w = sb("out_w", [P, P])
        out_c = sb("out_c", [P, P])
        beta_b = sb("beta_b", [P, P])
        neg_a = sb("neg_a", [P, N])

        x = sb("x", [P, C, D])
        xn = sb("xn", [P, C, D])
        xnT = sb("xnT", [P, B, BLEN])
        stats = sb("stats", [P, C, 6])
        mv = sb("mv", [P, C, 2])
        var_e = sb("var_e", [P, C])
        rstd = sb("rstd", [P, C])

        lg = sb("lg", [P, C, E])
        shared = sb("shared", [P, max(8 * GT, C * E * E + (T // GROUPS) * TOPK + 3 * J * NT // 2)])
        beats = shared[:, 0:C * E * E].rearrange("p (c e o) -> p c e o", c=C, e=E)
        rank = sb("rank", [P, C, E])
        top = sb("top", [P, TOPK, C, E])
        picked = sb("picked", [P, C + 1, E], BF16)
        prod = sb("prod", [P, TOPK, C, E])
        lsel = sb("lsel", [P, TOPK, C])
        ldiff = sb("ldiff", [P, C])
        e2 = sb("e2", [P, C])
        den = sb("den", [P, C])
        half_w = sb("half_w", [P, TOPK, C])
        over = sb("over", [P, E, C])
        ntile = sb("ntile", [P, E])
        tile_end = sb("tile_end", [P, E])
        base = sb("base", [P, E])
        slot = sb("slot", [P, C, E])
        slot_f = sb("slot_f", [P, J])
        slot_i = sb("slot_i", [P, J], I32)
        tile_i = sb("tile_i", [P, J], I32)
        row_i = sb("row_i", [P, J], I32)
        tile_f = sb("tile_f", [P, J])
        row_f = sb("row_f", [P, J])
        JP = J // GROUPS
        at_row, at_tile = C * E * E, C * E * E + JP * P
        at_ids = at_tile + J * NT // 2
        in_row = shared[:, at_row:at_tile].bitcast(BF16).rearrange("p (a j r) -> p a j r", a=2, j=JP)
        in_tile = shared[:, at_tile:at_ids].bitcast(BF16).rearrange("p (j t) -> p j t", j=J)
        ids_rhs = shared[:, at_ids:at_ids + J * NT].bitcast(BF16).rearrange("p (j v t) -> p j v t", j=J, v=2)
        ids = sb("ids", [P, 2, NT])
        id128 = sb("id128", [P, NT])
        empty = sb("empty", [P, NT])
        put_i = sb("put_i", [P, NT], I32)
        get_i = sb("get_i", [P, NT], I32)
        le_end = sb("le_end", [P, NT, E])
        exp_f = sb("exp_f", [P, NT])
        exp_i = sb("exp_i", [P, NT], I32)

        xg = sb("xg", [P, RING, D])
        xT_hi = sb("xT_hi", [P, RING, P], F32R)
        xT_lo = sb("xT_lo", [P, RING, P], F32R)
        gelu = sb("gelu", [P, F])
        hact = sb("hact", [P, F])
        hT_hi = sb("hT_hi", [P, RING, F], F32R)
        hT_lo = sb("hT_lo", [P, RING, F], F32R)
        ya = sb("ya", [P, D])
        ysb = sb("ysb", [P, RING, D])
        ybuf = staging[:].rearrange("p a b -> p (a b)")[:, 0:3 * 2 * GC * D].rearrange(
            "p (r k c d) -> p r k c d", r=3, k=TOPK, c=GC)

        gate = sb("gate", [P, T])
        delta = xn[:].rearrange("p c d -> p (c d)")
        hc = shared[:, 0:4 * GT].rearrange("p (r t) -> p r t", r=4)
        silu = shared[:, 4 * GT:6 * GT].rearrange("p (r t) -> p r t", r=2)
        soft = shared[:, 0:4 * GT]
        c_row = shared[:, 4 * GT:8 * GT].rearrange("p (r t) -> p r t", r=4)
        bc = sb("bc", [P, T], BF16)
        bc_rest = sb("bc_rest", [P, GT])
        rings = staging[:].rearrange("p a b -> p (a b)")[:, 0:6 * GT].rearrange("p (r t) -> p r t", r=6)
        bx, hs = rings[:, 0:2], rings[:, 2:6]

        consts_in_s, vectors_in_s, mats_in_s = sem("consts_loaded"), sem("vectors_loaded"), sem("mats_loaded")
        x_loaded = [sem(f"x_loaded_{g}") for g in range(GROUPS)]
        w_loaded = [sem(f"w_loaded_{i}") for i in range(2)]
        w_hi_done, w_lo_done = sem("w_hi_done"), sem("w_lo_done")
        dve_order, act_order, pool_order = sem("dve_order"), sem("act_order"), sem("pool_order")
        consts_ready = sem("consts_ready")
        setup_mm, setup_copied = sem("setup_mm"), sem("setup_copied")
        xnT_padded = sem("xnT_padded")
        var_ready, rstd_ready, xn_ready = sem("var_ready"), sem("rstd_ready"), sem("xn_ready")
        xn_turned, xnT_ready = sem("xn_turned"), sem("xnT_ready")
        xn_stored = [sem(f"xn_stored_{g}") for g in range(GROUPS)]
        logits_ready, ldiff_ready, e2_ready = sem("logits_ready"), sem("ldiff_ready"), sem("e2_ready")
        picked_ready, prefix_ready = sem("picked_ready"), sem("prefix_ready")
        onehot_ready, onehot_used = sem("onehot_ready"), sem("onehot_used")
        ids_ready, index_ready = sem("ids_ready"), sem("index_ready")
        gathered = [sem(f"gathered_{r}") for r in range(RING)]
        scattered = [sem(f"scattered_{r}") for r in range(RING)]
        x_turned, xT_hi_done, xT_ready = sem("x_turned"), sem("xT_hi_done"), sem("xT_ready")
        gate_done, gelu_done = sem("gate_done"), sem("gelu_done")
        up_done, hact_done = sem("up_done"), sem("hact_done")
        h_turned, hT_hi_done, hT_ready = sem("h_turned"), sem("hT_hi_done"), sem("hT_ready")
        down_done, ya_done, y_ready = sem("down_done"), sem("ya_done"), sem("y_ready")
        y_loaded = [sem(f"y_loaded_{i}") for i in range(3)]
        x_moved = sem("x_moved")
        xz_done, silu_done, gate_ready = sem("xz_done"), sem("silu_done"), sem("gate_ready")
        proj_done, abs_done, exp_done, log_done = sem("proj_done"), sem("abs_done"), sem("exp_done"), sem("log_done")
        pos_done = sem("pos_done")
        dg_ready, bc_hi_done, bc_rest_done, bc_mid_done, bc_ready = (
            sem("dg_ready"), sem("bc_hi_done"), sem("bc_rest_done"), sem("bc_mid_done"), sem("bc_ready"))
        cb_added = sem("cb_added")
        b_spread, c_spread, c_copied, decay_ready = sem("b_spread"), sem("c_spread"), sem("c_copied"), sem("decay_ready")
        bx_ready, h_ready, hc_ready, hc_summed = sem("bx_ready"), sem("h_ready"), sem("hc_ready"), sem("hc_summed")
        yT_ready, y_turned, out_done, out_added = sem("yT_ready"), sem("y_turned"), sem("out_done"), sem("out_added")
        yvar_ready, yrstd_ready = sem("yvar_ready"), sem("yrstd_ready")
        stored = sem("stored")

        def spread(ap, axis, shape):
            return ap.unsqueeze(axis).to_broadcast(shape)

        def batch_pair(q):
            return xnT[:, 2 * q:2 * q + 2, PAD:BLEN]

        def grp(g):
            return slice(g * GC, (g + 1) * GC)

        block = ctx.enter_context(nc.Block())

        @block.sync
        def _(sp):
            for g in range(GROUPS):
                sp.dma_start(x[:, grp(g), :], x_in[:, grp(g), :]).then_inc(x_loaded[g], 16)
                if g == 0:
                    sp.dma_start(consts[:], consts_in).then_inc(consts_in_s, 16)
            sp.dma_start(mats[:], mats_in).then_inc(mats_in_s, 16)
            sp.dma_start(vectors[:], vectors_in).then_inc(vectors_in_s, 16)
            for e in range(E):
                if e >= 2:
                    sp.wait_ge(w_hi_done, e - 1)
                    sp.wait_ge(w_lo_done, e - 1)
                sp.dma_start(staging[:, e % 2, :], experts_in[:, e, :]).then_inc(w_loaded[e % 2], 16)

            for l in range(2):
                rows = xn_dram[l].rearrange("(c p) d -> p c d", p=P)
                y_rows = y_dram[l].rearrange("(k c p) d -> p k c d", k=TOPK, p=P)
                for g in range(GROUPS):
                    sp.wait_ge(xn_ready, 2 * l * GROUPS + g + 1)
                    sp.dma_start(rows[:, grp(g), :], xn[:, grp(g), :]).then_inc(xn_stored[g], 16)
                for r in range(RING):
                    sp.wait_ge(scattered[r], 16 * (l + 1) * (NT // RING))
                for g in range(GROUPS):
                    if l or g == 3:
                        sp.wait_ge(x_moved, l * GROUPS + g - 2)
                    for k in range(TOPK):
                        sp.dma_start(ybuf[:, g % 3, k], y_rows[:, k, grp(g), :]).then_inc(y_loaded[g % 3], 16)
            for g in range(GROUPS):
                sp.wait_ge(x_moved, GROUPS + g + 1)
                sp.dma_start(out[:, grp(g), :], x[:, grp(g), :]).then_inc(stored, 16)
            sp.wait_ge(stored, 16 * GROUPS)

        @block.gpsimd
        def _(pool):
            order = [0]

            def chain(ins):
                order[0] += 1
                ins.then_inc(pool_order, 1)
                pool.wait_ge(pool_order, order[0])

            pool.memset(ones_b[:], 1.0)
            pool.memset(ones_f[:], 1.0)
            pool.memset(picked[:, C, :], 0.0)
            pool.memset(xnT[:, :, 0:PAD], 0.0).then_inc(xnT_padded, 1)
            chain(pool.memset(neg_half[:], -0.5))

            def rsqrt(g, source, value, done):
                v = slice(g * GC, (g + 1) * GC)
                pool.wait_ge(source, value)
                pool.tensor_tensor(rstd[:, v], var_e[:, v], neg_half[:, v], ALU.pow).then_inc(done, 1)

            def w_rest(e):
                pool.wait_ge(w_hi_done, e + 1)
                pool.tensor_tensor(w_lo[:, e, :], staging[:, e % 2, 0:GU], w_hi[:, e, :].bitcast(F32), ALU.subtract)
                pool.tensor_tensor(w_down[:, e, :, 1, :], staging[:, e % 2, GU:WCOLS].rearrange("p (f d) -> p f d", f=FC),
                                   w_down[:, e, :, 0, :].bitcast(F32), ALU.subtract).then_inc(w_lo_done, 1)

            def ffn(l):
                t0 = l * NT

                def get(t):
                    r = t % RING
                    if t >= RING:
                        pool.wait_ge(x_turned, t0 + t - RING + 1)
                    pool.indirect_dma_start(
                        out=xg[:, r, :], out_offset=None, in_=xn_dram[l],
                        in_offset=bass.IndirectOffsetOnAxis(ap=get_i[:, t:t + 1].bitcast(U32), axis=0),
                        bounds_check=T - 1, oob_is_err=False).then_inc(gathered[r], 16)

                def put(t):
                    pool.wait_ge(y_ready, t0 + t + 1)
                    pool.indirect_dma_start(
                        out=y_dram[l], in_=ysb[:, t % RING, :], in_offset=None,
                        out_offset=bass.IndirectOffsetOnAxis(ap=put_i[:, t:t + 1].bitcast(U32), axis=0),
                        bounds_check=TOPK * T - 1, oob_is_err=False).then_inc(scattered[t % RING], 16)

                pool.wait_ge(index_ready, l + 1)
                for g in range(GROUPS):
                    pool.wait_ge(xn_stored[g], 16 * (l + 1))
                for t in range(RING):
                    get(t)
                for t in range(RING, NT + RING):
                    if t < NT:
                        get(t)
                    if t >= 2 * RING:
                        put(t - 2 * RING)
                for t in range(NT - RING, NT):
                    put(t)

            def mamba():
                for g in range(GROUPS):
                    rsqrt(g, var_ready, GROUPS + g + 1, rstd_ready)
                pool.wait_ge(setup_copied, 3)
                pool.wait_ge(xn_ready, 2 * GROUPS)
                pool.tensor_tensor(x[:], x[:], spread(out_c[:], 1, [P, C, D]), ALU.add).then_inc(cb_added, 1)
                pool.wait_ge(cb_added, 1)
                for q in range(GROUPS):
                    cols = slice(q * GT, (q + 1) * GT)
                    pool.wait_ge(bc_rest_done, q + 1)
                    chain(pool.tensor_copy(bc[32:64, cols], bc_rest[32:64, :]))
                    pool.tensor_copy(bc[64:96, cols], bc_rest[64:96, :]).then_inc(bc_mid_done, 1)
                    pool.wait_ge(bc_mid_done, q + 1)
                    pool.tensor_tensor(bc[64:96, cols], bc_rest[64:96, :], bc[64:96, cols],
                                       ALU.subtract).then_inc(bc_ready, 1)
                    pool.wait_ge(bc_ready, q + 1)

                def step(k, n, ring_new):
                    pool.wait_ge(h_ready, k + 1)
                    pool.wait_ge(c_copied, k + 1)
                    if not ring_new:
                        pool.wait_ge(hc_summed, k - 3)
                    pool.tensor_tensor(hc[:, n % 4, :], hs[:, n % 4, :], c_row[:, n % 4, :],
                                       ALU.mult).then_inc(hc_ready, 1)

                for n in range(N):
                    step(n, n, n < 4)
                with pool.Fori(1, GROUPS) as q:
                    for n in range(N):
                        step(q * N + n, n, False)

            for g in range(GROUPS):
                rsqrt(g, var_ready, g + 1, rstd_ready)
            for e in range(E):
                w_rest(e)
            ffn(0)
            mamba()
            for g in range(GROUPS):
                rsqrt(g, yvar_ready, g + 1, yrstd_ready)
            for g in range(GROUPS):
                rsqrt(g, var_ready, 2 * GROUPS + g + 1, rstd_ready)
            ffn(1)

        @block.scalar
        def _(act):
            def copy_turned(s):
                for g in range(GROUPS):
                    copy_group(s, g)

            def copy_group(s, g):
                act.wait_ge(xn_turned, s * GROUPS + g + 1)
                nc.scalar.copy(batch_pair(g), ps[:, LNB[s] + g % 2, :].rearrange("p (b t) -> p b t", b=2)
                               ).then_inc(xnT_ready, 1)

            order = [0]
            LNB = (0, 4, 4)

            def split_weights(e):
                act.wait_ge(w_loaded[e % 2], 16 * (e // 2 + 1))
                nc.scalar.copy(w_hi[:, e, :], staging[:, e % 2, 0:GU])
                nc.scalar.copy(w_down[:, e, :, 0, :], staging[:, e % 2, GU:WCOLS].rearrange("p (f d) -> p f d", f=FC)
                               ).then_inc(w_hi_done, 1)

            def ffn(l):
                t0 = l * NT
                act.wait_ge(ldiff_ready, l + 1)
                nc.scalar.activation(e2[:], ldiff[:], ACT.Exp).then_inc(e2_ready, 1)

                def x_hi(t, r):
                    act.wait_ge(x_turned, t0 + t + 1)
                    if past(t0 + t - RING + 1):
                        act.wait_ge(up_done, t0 + t - RING + 1)
                    nc.scalar.copy(xT_hi[:, r, :], ps[:, 0, 0:P]).then_inc(xT_hi_done, 1)

                def act_gelu(t):
                    act.wait_ge(gate_done, t0 + t + 1)
                    if past(t0 + t):
                        act.wait_ge(hact_done, t0 + t)
                    nc.scalar.activation(gelu[:], ps[:, 1, :], ACT.Gelu).then_inc(gelu_done, 1)

                def h_hi(t, r):
                    act.wait_ge(h_turned, t0 + t + 1)
                    if past(t0 + t - RING + 1):
                        act.wait_ge(down_done, t0 + t - RING + 1)
                    nc.scalar.copy(hT_hi[:, r, :], ps[:, 3, :]).then_inc(hT_hi_done, 1)

                def y_first(t):
                    act.wait_ge(down_done, t0 + t + 1)
                    if past(t0 + t):
                        act.wait_ge(y_ready, t0 + t)
                    nc.scalar.copy(ya[:], ps[:, 4, 0:D]).then_inc(ya_done, 1)

                def step(i, r):
                    h_hi(i - 1, (r - 1) % RING)
                    act_gelu(i)
                    if not (isinstance(i, int) and i == NT - 1):
                        x_hi(i + 1, (r + 1) % RING)
                    if not (isinstance(i, int) and i == 1):
                        y_first(i - 2)

                x_hi(0, 0)
                act_gelu(0)
                x_hi(1, 1)
                tile_steps(act, step)
                h_hi(NT - 1, (NT - 1) % RING)
                y_first(NT - 2)
                y_first(NT - 1)

            def mamba():
                for q in range(GROUPS):
                    act.wait_ge(xz_done, q + 1)
                    if q >= 2:
                        act.wait_ge(gate_ready, q - 1)
                    nc.scalar.activation(silu[:, q % 2, :], ps[:, q % 2, :], ACT.Silu,
                                         bias=vectors[:, V_BCONV:V_BCONV + 1]).then_inc(silu_done, 1)
                for q in range(GROUPS):
                    cols = slice(q * GT, (q + 1) * GT)
                    act.wait_ge(proj_done, q + 1)
                    nc.scalar.activation(soft[:, cols], ps[:, 4 + q % 2, :], ACT.Abs,
                                         bias=vectors[:, V_BDT:V_BDT + 1]).then_inc(abs_done, 1)
                    nc.scalar.copy(bc[0:BCR, cols], ps[0:BCR, 6 + q % 2, :]).then_inc(bc_hi_done, 1)
                act.wait_ge(abs_done, GROUPS)
                nc.scalar.activation(soft, soft, ACT.Exp, scale=-1.0).then_inc(exp_done, 1)
                act.wait_ge(exp_done, 1)
                for q in range(GROUPS):
                    cols = slice(q * GT, (q + 1) * GT)
                    nc.scalar.activation(soft[:, cols], soft[:, cols], ACT.Ln, bias=1.0).then_inc(log_done, 1)

                def step(q, n, first):
                    k = q * N + n
                    if not first:
                        act.wait_ge(h_ready, k - 1)
                        if past(k - 3):
                            act.wait_ge(hc_ready, k - 3)
                    act.wait_ge(c_spread, k + 1)
                    nc.scalar.copy(c_row[:, n % 4, :], ps[:, 2 + n % 2, :]).then_inc(c_copied, 1)
                    nc.scalar.activation(ps[:, 4 + n % 2, :], delta[:, bass.ds(q * GT, GT)], ACT.Exp,
                                         scale=neg_a[:, n:n + 1]).then_inc(decay_ready, 1)

                act.wait_ge(dg_ready, GROUPS)
                for n in range(N):
                    step(0, n, n < 2)
                with act.Fori(1, GROUPS) as q:
                    for n in range(N):
                        step(q, n, False)

            split_weights(0)
            split_weights(1)
            copy_turned(0)
            for e in range(2, E):
                split_weights(e)
            act.wait_ge(setup_mm, 1)
            nc.scalar.copy(conv_w[:].rearrange("p a b -> p (a b)"), ps[:, 5, :]).then_inc(setup_copied, 1)
            act.wait_ge(setup_mm, 2)
            nc.scalar.copy(out_w[:], ps[:, 6, 0:P]).then_inc(setup_copied, 1)
            nc.scalar.activation(neg_a[:], vectors[:, V_ALOG:V_ALOG + N], ACT.Exp).then_inc(act_order, 1)
            order[0] += 1
            act.wait_ge(act_order, order[0])
            nc.scalar.mul(neg_a[:], neg_a[:], -1.0).then_inc(act_order, 1)
            order[0] += 1
            act.wait_ge(act_order, order[0])
            ffn(0)
            copy_turned(1)
            mamba()
            copy_turned(2)
            ffn(1)

        @block.tensor
        def _(pe):
            LNB = (0, 4, 4)

            def turn_group(s):
                for g in range(GROUPS):
                    pe.wait_ge(xn_ready, s * GROUPS + g + 1)
                    if g >= 2:
                        pe.wait_ge(xnT_ready, s * GROUPS + g - 1)
                    for c in range(GC):
                        t = pe.transpose(ps[:, LNB[s] + g % 2, c * P:(c + 1) * P], xn[:, g * GC + c, :], ident)
                    t.then_inc(xn_turned, 1)

            gu_hi, gu_lo = (w[:].rearrange("p e w -> p (e w)") for w in (w_hi, w_lo))
            dn_hi_lo = w_down[:].rearrange("p e f s d -> p (e f s d)")

            def split_product(acc, x_hi, x_lo, w_cols):
                pe.matmul(acc, x_hi, gu_hi[:, w_cols], start=True, stop=False)
                pe.matmul(acc, x_hi, gu_lo[:, w_cols], start=False, stop=False)
                return pe.matmul(acc, x_lo, gu_hi[:, w_cols], start=False, stop=True)

            def route(l):
                for g in range(GROUPS):
                    pe.wait_ge(xnT_ready, 2 * l * GROUPS + g + 1)
                    for c in range(GC):
                        at = 2 * g + c // 2, PAD + (c % 2) * P
                        m = pe.matmul(ps[:, 2, (g * GC + c) * E:(g * GC + c + 1) * E],
                                      xnT[:, at[0], at[1]:at[1] + P], mats[:, M_GATE:M_GATE + E],
                                      start=True, stop=True)
                m.then_inc(logits_ready, 1)
                pe.wait_ge(picked_ready, l + 1)
                flat = picked[:].rearrange("p c e -> p (c e)")
                w = (C + 1) * E
                pe.matmul(ps[:, 3, 0:w], tri_b[:], flat, start=True, stop=False)
                for s in range(1, C + 1):
                    m = pe.matmul(ps[:, 3, s * E:w], ones_b[:], flat[:, 0:w - s * E], start=False, stop=(s == C))
                m.then_inc(prefix_ready, 1)
                for g in range(GROUPS):
                    pe.wait_ge(onehot_ready, l * GROUPS + g + 1)
                    for i in range(JP):
                        j = g * JP + i
                        m = pe.matmul(ps[:, 4, 0:2 * NT], in_row[:, g % 2, i, :],
                                      ids_rhs[:, j].rearrange("p v t -> p (v t)"), start=(j == 0), stop=(j == J - 1))
                    m.then_inc(onehot_used, 1)

            def ffn(l):
                t0 = l * NT

                def turn_x(t, r, n):
                    pe.wait_ge(gathered[r], (l * (NT // RING) + n + 1) * 16)
                    if past(t0 + t):
                        pe.wait_ge(xT_ready, t0 + t)
                    pe.transpose(ps[:, 0, 0:P], xg[:, r, :], ident).then_inc(x_turned, 1)

                def gate_p(t, r):
                    pe.wait_ge(xT_ready, t0 + t + 1)
                    if past(t0 + t):
                        pe.wait_ge(gelu_done, t0 + t)
                    split_product(ps[:, 1, :], xT_hi[:, r, :], xT_lo[:, r, :],
                                  bass.ds(expert(r) * GU, F)).then_inc(gate_done, 1)

                def up_p(t, r):
                    if past(t0 + t):
                        pe.wait_ge(hact_done, t0 + t)
                    split_product(ps[:, 2, :], xT_hi[:, r, :], xT_lo[:, r, :],
                                  bass.ds(expert(r) * GU + F, F)).then_inc(up_done, 1)

                def turn_h(t):
                    pe.wait_ge(hact_done, t0 + t + 1)
                    if past(t0 + t):
                        pe.wait_ge(hT_ready, t0 + t)
                    for f in range(FC):
                        m = pe.transpose(ps[:, 3, f * P:(f + 1) * P], hact[:, f * P:(f + 1) * P], ident)
                    m.then_inc(h_turned, 1)

                def down_p(t, r):
                    pe.wait_ge(hT_ready, t0 + t + 1)
                    if past(t0 + t):
                        pe.wait_ge(y_ready, t0 + t)
                    for f in range(FC):
                        w = expert(r) * (2 * FC * D) + 2 * f * D
                        pe.matmul(ps[:, 4, 0:2 * D], hT_hi[:, r, f * P:(f + 1) * P], dn_hi_lo[:, bass.ds(w, 2 * D)],
                                  start=(f == 0), stop=False, skip_group_check=True)
                        m = pe.matmul(ps[:, 4, 0:D], hT_lo[:, r, f * P:(f + 1) * P], dn_hi_lo[:, bass.ds(w, D)],
                                      start=False, stop=(f == FC - 1), skip_group_check=True)
                    m.then_inc(down_done, 1)

                def read_expert(t, r):
                    pe.reg_load(expert_reg[r], exp_i[0:1, bass.ds(t, 1)])

                def expert(r):
                    return pe.snap(expert_reg[r], min_val=0, max_val=E - 1)

                pe.wait_ge(index_ready, l + 1)
                pe.wait_ge(w_lo_done, E)
                read_expert(0, 0)
                read_expert(1, 1)
                turn_x(0, 0, 0)
                gate_p(0, 0)
                up_p(0, 0)
                turn_x(1, 1, 0)

                def step(i, r):
                    turn_h(i - 1)
                    gate_p(i, r)
                    up_p(i, r)
                    after, before = (r + 1) % RING, (r + 1) % RING
                    if not (isinstance(i, int) and i == NT - 1):
                        n = (i + 1) // RING if isinstance(i, int) else turns_before(i, r)
                        turn_x(i + 1, after, n)
                    if not (isinstance(i, int) and i == 1):
                        down_p(i - 2, before)
                    if not (isinstance(i, int) and i == NT - 1):
                        read_expert(i + 1, after)

                def turns_before(i, r):
                    return loop_m[0] + (HEAD + (r - HEAD) % RING + 1) // RING

                loop_m = [None]
                for i in range(1, HEAD):
                    step(i, i % RING)
                with pe.Fori(0, LOOPS) as m:
                    loop_m[0] = m
                    for u in range(RING):
                        step(m * RING + (HEAD + u), (HEAD + u) % RING)
                step(NT - 1, (NT - 1) % RING)
                turn_h(NT - 1)
                down_p(NT - 2, (NT - 2) % RING)
                down_p(NT - 1, (NT - 1) % RING)

            def mamba():
                for q in range(GROUPS):
                    if q >= 2:
                        pe.wait_ge(gate_ready, q - 1)
                    pe.wait_ge(xnT_ready, GROUPS + q + 1)
                    for k in range(TAPS):
                        pe.matmul(ps[:, q % 2, :], conv_w[:, k, :], xnT[:, 2 * q:2 * q + 2, PAD - TAPS + 1 + k:PAD - TAPS + 1 + k + L],
                                  start=(k == 0), stop=(k == TAPS - 1))
                    pe.matmul(ps[:, 2 + q % 2, :], mats[:, M_INZ:M_INZ + D], batch_pair(q),
                              start=True, stop=True).then_inc(xz_done, 1)
                for q in range(GROUPS):
                    cols = slice(q * GT, (q + 1) * GT)
                    pe.wait_ge(gate_ready, q + 1)
                    if q >= 2:
                        pe.wait_ge(pos_done, q - 1)
                        pe.wait_ge(bc_rest_done, q - 1)
                    pe.matmul(ps[:, 4 + q % 2, :], mats[:, M_DT:M_DT + D], gate[:, cols], start=True, stop=True)
                    pe.matmul(ps[0:BCR, 6 + q % 2, :], mats[:, M_BC:M_BC + BCR], gate[:, cols],
                              start=True, stop=True).then_inc(proj_done, 1)

                def spread_bc(q, n, first):
                    k = q * N + n
                    if not first:
                        pe.wait_ge(bx_ready, k - 1)
                    pe.matmul(ps[:, n % 2, :], sel_b[0:BCR, n:n + 1].to_broadcast([BCR, P]),
                              bc[0:BCR, bass.ds(q * GT, GT)], start=True, stop=True).then_inc(b_spread, 1)
                    if not first:
                        pe.wait_ge(c_copied, k - 1)
                    pe.matmul(ps[:, 2 + n % 2, :], sel_b[0:BCR, N + n:N + n + 1].to_broadcast([BCR, P]),
                              bc[0:BCR, bass.ds(q * GT, GT)], start=True, stop=True).then_inc(c_spread, 1)

                def sum_states(q, n, first):
                    k = q * N + n
                    pe.wait_ge(hc_ready, k + 1)
                    if n == 0 and not first:
                        pe.wait_ge(yT_ready, q)
                    pe.matmul(ps[:, 6, :], ident, hc[:, n % 4, :], start=(n == 0), stop=(n == N - 1)
                              ).then_inc(hc_summed, 1)

                pe.wait_ge(bc_ready, GROUPS)
                for n in range(LAG):
                    spread_bc(0, n, n < 2)
                for n in range(N):
                    sum_states(0, n, True)
                    spread_bc((n + LAG) // N, (n + LAG) % N, False)
                with pe.Fori(1, GROUPS - 1) as q:
                    for n in range(N):
                        sum_states(q, n, False)
                        spread_bc(q + (n + LAG) // N, (n + LAG) % N, False)
                for n in range(N):
                    sum_states(GROUPS - 1, n, False)
                    if n + LAG < N:
                        spread_bc(GROUPS - 1, n + LAG, False)

                for q in range(GROUPS):
                    pe.wait_ge(yT_ready, q + 1)
                    if q >= 2:
                        pe.wait_ge(out_added, q - 1)
                    for c in range(GC):
                        m = pe.transpose(ps[:, q % 2, c * P:(c + 1) * P], xnT[:, 2 * q + c // 2, PAD + (c % 2) * P:PAD + (c % 2) * P + P], ident)
                    m.then_inc(y_turned, 1)
                    for c in range(GC):
                        m = pe.matmul(ps[:, 2 + q % 2, c * P:(c + 1) * P], xnT[:, 2 * q + c // 2, PAD + (c % 2) * P:PAD + (c % 2) * P + P],
                                      out_w[:], start=True, stop=True)
                    m.then_inc(out_done, 1)

            expert_reg = [pe.alloc_register(f"expert_{r}") for r in range(RING)]
            pe.wait_ge(consts_in_s, 16)
            turn_group(0)
            pe.wait_ge(mats_in_s, 16)
            pe.wait_ge(consts_ready, 1)
            for k in range(TAPS):
                m = pe.transpose(ps[:, 5, k * P:(k + 1) * P], conv_rows[:, k, :], ident)
            m.then_inc(setup_mm, 1)
            pe.matmul(ps[:, 6, 0:P], consts[:, K_CENTRE:K_CENTRE + P], out_g[:], start=True, stop=True).then_inc(setup_mm, 1)
            pe.matmul(ps[:, 7, 0:P], beta_b[:], mats[:, M_OUT:M_OUT + D], start=True, stop=True).then_inc(setup_mm, 1)
            route(0)
            ffn(0)
            turn_group(1)
            mamba()
            turn_group(2)
            route(1)
            ffn(1)

        @block.vector
        def _(dve):
            order = [0]

            def chain(ins):
                order[0] += 1
                ins.then_inc(dve_order, 1)
                dve.wait_ge(dve_order, order[0])

            def statistics(rows, g, ready_sem):
                for c in range(GC):
                    i = dve.bn_stats(stats[:, g * GC + c, :], rows(c))
                chain(i)
                for c in range(GC):
                    i = dve.bn_aggr(mv[:, g * GC + c, :], stats[:, g * GC + c, :])
                chain(i)
                dve.tensor_scalar(var_e[:, grp(g)], mv[:, grp(g), 1], EPS, None, ALU.add).then_inc(ready_sem, 1)

            def normalise(s, arrive):
                for g in range(GROUPS + 1):
                    if g < GROUPS:
                        arrive(g)
                        statistics(lambda c: x[:, g * GC + c, :], g, var_ready)
                    if g >= 1:
                        h = g - 1
                        dve.wait_ge(rstd_ready, s * GROUPS + h + 1)
                        if s:
                            dve.wait_ge(xn_stored[h], 16)
                        for c in range(h * GC, (h + 1) * GC):
                            i = dve.tensor_scalar(xn[:, c, :], x[:, c, :], mv[:, c, 0:1], rstd[:, c:c + 1],
                                                  ALU.subtract, ALU.mult)
                        i.then_inc(xn_ready, 1)

            def route(l):
                dve.wait_ge(logits_ready, l + 1)
                chain(dve.tensor_copy(lg[:].rearrange("p c e -> p (c e)"), ps[:, 2, 0:C * E]))
                dve.memset(shared[:, 0:C * E * E].rearrange("p (c o) -> p c o", c=C)[:, :, 0:E * E:E + 1], 0.0)
                for e in range(E):
                    if e:
                        i = dve.tensor_tensor(beats[:, :, e, 0:e], lg[:, :, 0:e],
                                              lg[:, :, e:e + 1].to_broadcast([P, C, e]), ALU.is_ge)
                    if e < E - 1:
                        i = dve.tensor_tensor(beats[:, :, e, e + 1:E], lg[:, :, e + 1:E],
                                              lg[:, :, e:e + 1].to_broadcast([P, C, E - 1 - e]), ALU.is_gt)
                chain(i)
                chain(dve.tensor_reduce(rank[:], beats[:], AX.X, ALU.add))
                dve.tensor_scalar(picked[:, 0:C, :], rank[:], 2.0, None, ALU.is_lt).then_inc(picked_ready, 1)
                dve.tensor_scalar(top[:, 0], rank[:], 0.0, None, ALU.is_equal)
                chain(dve.tensor_scalar(top[:, 1], rank[:], 1.0, None, ALU.is_equal))
                chain(dve.tensor_tensor(prod[:], top[:], spread(lg[:], 1, [P, TOPK, C, E]), ALU.mult))
                chain(dve.tensor_reduce(lsel[:], prod[:], AX.X, ALU.add))
                dve.tensor_tensor(ldiff[:], lsel[:, 1], lsel[:, 0], ALU.subtract).then_inc(ldiff_ready, 1)

                dve.wait_ge(prefix_ready, l + 1)
                counts = ps[:, 3, C * E:(C + 1) * E]
                chain(dve.tensor_tensor(over[:], spread(counts, 2, [P, E, C]),
                                        spread(consts[:, K_TILE:K_TILE + C], 1, [P, E, C]), ALU.is_gt))
                chain(dve.tensor_reduce(ntile[:], over[:], AX.X, ALU.add))
                chain(dve.tensor_tensor_scan(tile_end[:], ones_f[:], ntile[:], 0.0, ALU.mult, ALU.add))
                chain(dve.tensor_tensor(base[:], tile_end[:], ntile[:], ALU.subtract))
                chain(dve.tensor_scalar(base[:], base[:], float(P), None, ALU.mult))
                chain(dve.tensor_tensor(slot[:], ps[:, 3, 0:C * E].rearrange("p (c e) -> p c e", e=E),
                                        spread(base[:], 1, [P, C, E]), ALU.add))
                chain(dve.tensor_tensor(prod[:], top[:], spread(slot[:], 1, [P, TOPK, C, E]), ALU.mult))
                chain(dve.tensor_reduce(slot_f[:].rearrange("p (k c) -> p k c", k=TOPK), prod[:], AX.X, ALU.add))
                chain(dve.tensor_copy(slot_i[:], slot_f[:]))
                dve.tensor_scalar(tile_i[:], slot_i[:], P.bit_length() - 1, None, ALU.arith_shift_right)
                chain(dve.tensor_scalar(row_i[:], slot_i[:], P - 1, None, ALU.bitwise_and))
                dve.tensor_copy(tile_f[:], tile_i[:])
                chain(dve.tensor_copy(row_f[:], row_i[:]))
                iota = consts[:, K_IOTA:K_IOTA + P]
                chain(dve.tensor_tensor(in_tile[:], spread(iota[:, 0:NT], 1, [P, J, NT]),
                                        spread(tile_f[:], 2, [P, J, NT]), ALU.is_equal))
                dve.tensor_tensor(ids_rhs[:, :, 0, :], in_tile[:],
                                  spread(consts[:, K_JP1:K_JP1 + J], 2, [P, J, NT]), ALU.mult)
                dve.tensor_scalar(ids_rhs[:, :, 1, :], in_tile[:], consts[:, K_P:K_P + 1], None, ALU.mult)
                for g in range(GROUPS):
                    if l or g >= 2:
                        dve.wait_ge(onehot_used, l * GROUPS + g - 1)
                    dve.tensor_tensor(in_row[:, g % 2], spread(iota, 1, [P, JP, P]),
                                      spread(row_f[:, g * JP:(g + 1) * JP], 2, [P, JP, P]),
                                      ALU.is_equal).then_inc(onehot_ready, 1)
                chain(dve.tensor_tensor(le_end[:], spread(iota[:, 0:NT], 2, [P, NT, E]),
                                        spread(tile_end[:], 1, [P, NT, E]), ALU.is_ge))
                chain(dve.tensor_reduce(exp_f[:], le_end[:], AX.X, ALU.add))
                dve.tensor_scalar(exp_i[:], exp_f[:], float(E - 1), None, ALU.min)
                dve.wait_ge(e2_ready, l + 1)
                chain(dve.tensor_scalar(den[:], e2[:], 1.0, None, ALU.add))
                chain(dve.reciprocal(den[:], den[:]))
                dve.tensor_scalar(half_w[:, 0], den[:], 0.5, None, ALU.mult)
                chain(dve.tensor_tensor(half_w[:, 1], den[:], e2[:], ALU.mult))
                chain(dve.tensor_scalar(half_w[:, 1], half_w[:, 1], 0.5, None, ALU.mult))
                dve.wait_ge(onehot_used, (l + 1) * GROUPS)
                chain(dve.tensor_copy(ids[:].rearrange("p v t -> p (v t)"), ps[:, 4, 0:2 * NT]))
                chain(dve.scalar_tensor_tensor(out=id128[:], in0=ids[:, 0], scalar=float(P), in1=ids[:, 1],
                                               op0=ALU.mult, op1=ALU.add))
                chain(dve.tensor_scalar(empty[:], id128[:], 1.0, float(TOPK * T + P), ALU.is_lt, ALU.mult))
                chain(dve.scalar_tensor_tensor(out=put_i[:], in0=empty[:], scalar=-float(P), in1=id128[:],
                                               op0=ALU.add, op1=ALU.add))
                dve.tensor_scalar(get_i[:], put_i[:], T - 1, None, ALU.bitwise_and).then_inc(index_ready, 1)

            def ffn(l):
                t0 = l * NT

                def x_lo(t, r):
                    dve.wait_ge(xT_hi_done, t0 + t + 1)
                    if past(t0 + t - RING + 1):
                        dve.wait_ge(up_done, t0 + t - RING + 1)
                    dve.tensor_tensor(xT_lo[:, r, :], ps[:, 0, 0:P], xT_hi[:, r, :].bitcast(F32),
                                      ALU.subtract).then_inc(xT_ready, 1)

                def h_act(t):
                    dve.wait_ge(up_done, t0 + t + 1)
                    dve.wait_ge(gelu_done, t0 + t + 1)
                    if past(t0 + t):
                        dve.wait_ge(h_turned, t0 + t)
                    dve.tensor_tensor(hact[:], ps[:, 2, :], gelu[:], ALU.mult).then_inc(hact_done, 1)

                def h_lo(t, r):
                    dve.wait_ge(hT_hi_done, t0 + t + 1)
                    if past(t0 + t - RING + 1):
                        dve.wait_ge(down_done, t0 + t - RING + 1)
                    dve.tensor_tensor(hT_lo[:, r, :], ps[:, 3, :], hT_hi[:, r, :].bitcast(F32),
                                      ALU.subtract).then_inc(hT_ready, 1)

                def y_sum(t, r, n):
                    dve.wait_ge(ya_done, t0 + t + 1)
                    if past(l * (NT // RING) + n):
                        dve.wait_ge(scattered[r], (l * (NT // RING) + n) * 16)
                    dve.tensor_tensor(ysb[:, r, :], ps[:, 4, D:2 * D], ya[:], ALU.add).then_inc(y_ready, 1)

                def step(i, r, m=None):
                    h_lo(i - 1, (r - 1) % RING)
                    h_act(i)
                    if not (isinstance(i, int) and i == NT - 1):
                        x_lo(i + 1, (r + 1) % RING)
                    if not (isinstance(i, int) and i == 1):
                        n = (i - 2) // RING if m is None else m + (HEAD + (r - HEAD) % RING - 2) // RING
                        y_sum(i - 2, (r - 2) % RING, n)

                x_lo(0, 0)
                h_act(0)
                x_lo(1, 1)
                for i in range(1, HEAD):
                    step(i, i % RING)
                with dve.Fori(0, LOOPS) as m:
                    for u in range(RING):
                        step(m * RING + (HEAD + u), (HEAD + u) % RING, m)
                step(NT - 1, (NT - 1) % RING)
                h_lo(NT - 1, (NT - 1) % RING)
                y_sum(NT - 2, (NT - 2) % RING, (NT - 2) // RING)
                y_sum(NT - 1, (NT - 1) % RING, (NT - 1) // RING)

            def add_experts(l, g):
                loads = sum(1 for i in range(l * GROUPS + g + 1) if i % GROUPS % 3 == g % 3)
                dve.wait_ge(y_loaded[g % 3], 16 * TOPK * loads)
                for k in range(TOPK):
                    for c in range(GC):
                        at = g * GC + c
                        i = dve.scalar_tensor_tensor(out=x[:, at, :], in0=ybuf[:, g % 3, k, c, :],
                                                     scalar=half_w[:, k, at:at + 1], in1=x[:, at, :],
                                                     op0=ALU.mult, op1=ALU.add)
                    if k == 0:
                        chain(i)
                i.then_inc(x_moved, 1)
                dve.wait_ge(x_moved, l * GROUPS + g + 1)

            def mamba():
                for q in range(GROUPS):
                    dve.wait_ge(silu_done, q + 1)
                    dve.tensor_tensor(gate[:, q * GT:(q + 1) * GT], ps[:, 2 + q % 2, :], silu[:, q % 2, :],
                                      ALU.mult).then_inc(gate_ready, 1)
                for q in range(GROUPS):
                    cols = slice(q * GT, (q + 1) * GT)
                    dve.wait_ge(bc_hi_done, q + 1)
                    if q:
                        dve.wait_ge(bc_ready, q)
                    dve.tensor_tensor(bc_rest[32:64, :], ps[32:64, 6 + q % 2, :], bc[32:64, cols], ALU.subtract)
                    dve.tensor_tensor(bc_rest[64:96, :], ps[64:96, 6 + q % 2, :], bc[64:96, cols],
                                      ALU.subtract).then_inc(bc_rest_done, 1)
                    dve.wait_ge(abs_done, q + 1)
                    dve.tensor_scalar(delta[:, cols], ps[:, 4 + q % 2, :], vectors[:, V_BDT:V_BDT + 1], 0.0,
                                      ALU.add, ALU.max).then_inc(pos_done, 1)
                for q in range(GROUPS):
                    cols = slice(q * GT, (q + 1) * GT)
                    dve.wait_ge(log_done, q + 1)
                    chain(dve.tensor_tensor(delta[:, cols], delta[:, cols], soft[:, cols], ALU.add))
                    dve.tensor_tensor(gate[:, cols], gate[:, cols], delta[:, cols], ALU.mult).then_inc(dg_ready, 1)

                def y_add(q):
                    dve.wait_ge(hc_summed, (q + 1) * N)
                    at = xnT[:, bass.ds(q * 2, 2), PAD:BLEN]
                    dve.tensor_tensor(at, ps[:, 6, :].rearrange("p (b t) -> p b t", b=2), at,
                                      ALU.add).then_inc(yT_ready, 1)

                def step(q, n, first):
                    k = q * N + n
                    dve.wait_ge(b_spread, k + 1)
                    dve.tensor_tensor(bx[:, n % 2, :], ps[:, n % 2, :], gate[:, bass.ds(q * GT, GT)],
                                      ALU.mult).then_inc(bx_ready, 1)
                    dve.wait_ge(bx_ready, k + 1)
                    dve.wait_ge(decay_ready, k + 1)
                    if not first and past(k - 3):
                        dve.wait_ge(hc_ready, k - 3)
                    for b in range(2):
                        t = slice(b * L, (b + 1) * L)
                        i = dve.tensor_tensor_scan(hs[:, n % 4, t], ps[:, 4 + n % 2, t], bx[:, n % 2, t], 0.0,
                                                   ALU.mult, ALU.add)
                    i.then_inc(h_ready, 1)

                dve.wait_ge(dg_ready, GROUPS)
                for n in range(N):
                    step(0, n, n < 2)
                with dve.Fori(1, GROUPS) as q:
                    for n in range(N):
                        step(q, n, False)
                        if n == 2:
                            y_add(q - 1)
                y_add(GROUPS - 1)
                dve.wait_ge(cb_added, 1)
                for q in range(GROUPS):
                    dve.wait_ge(y_turned, q + 1)
                    statistics(lambda c: ps[:, q % 2, c * P:(c + 1) * P], q, yvar_ready)
                    dve.wait_ge(yrstd_ready, q + 1)
                    dve.wait_ge(out_done, q + 1)
                    for c in range(GC):
                        at = q * GC + c
                        i = dve.scalar_tensor_tensor(out=x[:, at, :], in0=ps[:, 2 + q % 2, c * P:(c + 1) * P],
                                                     scalar=rstd[:, at:at + 1], in1=x[:, at, :],
                                                     op0=ALU.mult, op1=ALU.add)
                    i.then_inc(out_added, 1)

            dve.wait_ge(consts_in_s, 16)
            dve.tensor_copy(tri_b[:], consts[:, K_TRI:K_TRI + P])
            dve.tensor_copy(sel_b[:], consts[:, K_SEL:K_SEL + 2 * N])
            normalise(0, lambda g: dve.wait_ge(x_loaded[g], 16))
            dve.wait_ge(mats_in_s, 16)
            dve.wait_ge(vectors_in_s, 16)
            dve.wait_ge(xnT_padded, 1)
            for k in range(TAPS):
                dve.tensor_scalar(conv_rows[:, k, :], mats[:, M_INX:M_INX + D], vectors[:, V_CONV + k:V_CONV + k + 1],
                                  None, ALU.mult)
            dve.tensor_scalar(out_g[:], mats[:, M_OUT:M_OUT + D], vectors[:, V_GAMMA:V_GAMMA + 1], None, ALU.mult)
            dve.tensor_copy(beta_b[:], vectors[:, V_BETA:V_BETA + 1].to_broadcast([P, P])).then_inc(consts_ready, 1)
            route(0)
            dve.wait_ge(setup_mm, 3)
            dve.tensor_tensor(out_c[:], ps[:, 7, 0:P], mats[:, M_BOUT:M_BOUT + D], ALU.add).then_inc(setup_copied, 1)
            ffn(0)
            normalise(1, lambda g: add_experts(0, g))
            mamba()
            normalise(2, lambda g: dve.wait_ge(out_added, g + 1))
            route(1)
            ffn(1)
            for g in range(GROUPS):
                add_experts(1, g)


_INS = ["x_rows", "experts", "consts", "vectors", "mats"]


def _constants():
    import numpy as np

    k = np.zeros((P, K_COLS), np.float32)
    i = np.arange(P)
    k[:, K_IOTA:K_IOTA + P] = i
    k[:, K_TRI:K_TRI + P] = i[:, None] < i[None, :]
    k[:, K_CENTRE:K_CENTRE + P] = np.eye(P) - 1.0 / P
    k[:, K_IDENT:K_IDENT + P] = np.eye(P)
    k[:, K_TILE:K_TILE + C] = P * np.arange(C)
    k[:, K_JP1:K_JP1 + J] = np.arange(J) + 1
    k[:, K_P] = i
    k[:, K_SEL:K_SEL + 2 * N] = (i[:, None] % (2 * N)) == np.arange(2 * N)
    return k


def kernel(**inputs):
    import numpy as np
    import concourse.bacc as bacc
    from concourse.bass_utils import run_bass_kernel_spmd

    a = {k.split("_", 2)[2]: np.asarray(v) for k, v in inputs.items()}
    col = lambda v: v.reshape(P, -1)
    gu = a["gate_up_w"].transpose(2, 0, 1)
    dn = a["down_w"].reshape(E, D, FC, P).transpose(3, 0, 2, 1).reshape(P, E, FC * D)
    arrays = {
        "x_rows": a["x"].reshape(C, P, D).transpose(1, 0, 2),
        "experts": np.concatenate([gu, dn], axis=2),
        "consts": _constants(),
        "vectors": np.concatenate([col(a["b_conv"]), col(a["b_dt"]), col(a["ln_gamma"]), col(a["ln_beta"]),
                                   a["W_conv"].reshape(D, TAPS), a["A_log"]], axis=1),
        "mats": np.concatenate([a["W_in"][:D], a["W_in"][D:].T, a["W_dt"].T, a["W_out"].T,
                                np.broadcast_to(a["b_out"], (P, D))] + [a["W_xproj"].T] * BC_PARTS
                               + [a["gate_w"].T], axis=1),
    }
    arrays = {k: np.ascontiguousarray(v) for k, v in arrays.items()}
    nc = bacc.Bacc("TRN2", target_bir_lowering=False, num_devices=1)
    args = [nc.dram_tensor(f"in_{k}", arrays[k].shape, mybir.dt.from_np(arrays[k].dtype), kind="ExternalInput").ap()
            for k in _INS]
    args.append(nc.dram_tensor("out_rows", (P, C, D), F32, kind="ExternalOutput").ap())
    macaron_block(nc, *args)
    r = run_bass_kernel_spmd(nc, [{f"in_{k}": arrays[k] for k in _INS}], core_ids=[0])
    return r.results[0]["out_rows"].transpose(1, 0, 2).reshape(B, L, D)
```
